# Optimizing a Trainium2 kernel written in Bass

```python
import numpy as np
import jax
import jax.numpy as jnp

def _softmax(x, axis=-1):
    return jax.nn.softmax(x, axis=axis)

def _gelu(x):
    return jax.nn.gelu(x, approximate=True)

def _silu(x):
    return jax.nn.silu(x)

def _sigmoid(x):
    return jax.nn.sigmoid(x)

def _layernorm(x, axis=-1, eps=1e-05):
    m = jnp.mean(x, axis=axis, keepdims=True)
    v = jnp.var(x, axis=axis, keepdims=True)
    return (x - m) / jnp.sqrt(v + eps)

def _scatter_add(tgt, idx, src, axis=0):
    return tgt.at[idx].add(src)

def _segment_sum(src, seg, n):
    return jax.ops.segment_sum(src, seg, n)
kernel_name = 'mk_gnn_resnorm_d2_gnn_r8_73d3f7'

def setup_inputs(seed: int=0):
    np.random.seed(seed)
    _w = jnp.asarray

    def _rec_inputs():
        import jax
        import jax.numpy as jnp
        _gk = jax.random.key(seed)
        x = -0.000202 + 1 * jax.random.normal(jax.random.fold_in(_gk, 1), (6250, 128), jnp.float32)
        _s = jax.random.randint(jax.random.fold_in(_gk, 2), (50000,), 0, 6250, jnp.int32)
        _d = jax.random.randint(jax.random.fold_in(_gk, 3), (50000,), 0, 6250, jnp.int32)
        _loop = jnp.arange(6250, dtype=jnp.int32)
        src = jnp.concatenate([_s, _d, _loop])
        dst = jnp.concatenate([_d, _s, _loop])
        _o = jnp.argsort(dst, stable=True)
        src = src[_o]
        dst = dst[_o]
        edge_type_40 = jax.random.randint(jax.random.fold_in(_gk, 13), (106250,), 0, 40, jnp.int32)
        edge_weight = jax.random.uniform(jax.random.fold_in(_gk, 14), (106250,), jnp.float32, 0.0, 0.0625)
        return (x, src, dst, edge_type_40, edge_weight)
    x, src, dst, edge_type_40, edge_weight = _rec_inputs()

    def _L0_gnn_setup():
        import jax, jax.numpy as jnp
        import numpy as np
        N, E, D, R = (6250, 200000, 128, 40)
        DIFFUSION_STEPS = 1
        key = jax.random.key(seed)
        ks = jax.random.split(key, 8)
        return {'h': jax.random.normal(ks[0], (N, D), dtype=jnp.float32), 'rFeatures': jax.random.normal(ks[1], (R, D), dtype=jnp.float32), 'relation_weights': jax.random.normal(ks[2], (R, D, D), dtype=jnp.float32) * (1.0 / np.sqrt(D)), 'loop_weight': jax.random.normal(ks[3], (D, D), dtype=jnp.float32) * (1.0 / np.sqrt(D)), 'norm': jax.random.uniform(ks[4], (N, 1), dtype=jnp.float32), 'edge_src': jax.random.randint(ks[5], (E,), 0, N, dtype=jnp.int32), 'edge_dst': jax.random.randint(ks[6], (E,), 0, N, dtype=jnp.int32), 'edge_type': jax.random.randint(ks[7], (E,), 0, R, dtype=jnp.int32)}
    _L0_gnn_all = _L0_gnn_setup()
    _L0_gnn_in = {k: v for k, v in _L0_gnn_all.items() if k in ('rFeatures', 'relation_weights', 'loop_weight')}
    del _L0_gnn_all

    def _L1_gnn_setup():
        import jax, jax.numpy as jnp
        import numpy as np
        N = 12500
        E = 200000
        D = 128
        NEG_SLOPE = 0.2
        EPS = 1e-12
        key = jax.random.key(seed)
        k1, k2, k3, k4, k5, k6 = jax.random.split(key, 6)
        ego = jax.random.normal(k1, (N, D), dtype=jnp.float32)
        std = float(np.sqrt(2.0 / (D + D)))
        W1 = jax.random.normal(k2, (D, D), dtype=jnp.float32) * std
        W2 = jax.random.normal(k3, (D, D), dtype=jnp.float32) * std
        b1 = jnp.zeros((1, D), dtype=jnp.float32)
        b2 = jnp.zeros((1, D), dtype=jnp.float32)
        src = jax.random.randint(k4, (E,), 0, N)
        dst = jax.random.randint(k5, (E,), 0, N)
        adj_vals = jax.random.uniform(k6, (E,), dtype=jnp.float32) * (1.0 / 16.0)
        return {'ego_embeddings': ego, 'W1': W1, 'W2': W2, 'b1': b1, 'b2': b2, 'adj_vals': adj_vals, 'src': src, 'dst': dst}
    _L1_gnn_all = _L1_gnn_setup()
    _L1_gnn_in = {k: v for k, v in _L1_gnn_all.items() if k in ('W1', 'W2', 'b1', 'b2')}
    del _L1_gnn_all
    return {'x': x, 'src': src, 'dst': dst, 'edge_type_40': edge_type_40, 'edge_weight': edge_weight, 'L0_gnn_rFeatures': _L0_gnn_in['rFeatures'], 'L0_gnn_relation_weights': _L0_gnn_in['relation_weights'], 'L0_gnn_loop_weight': _L0_gnn_in['loop_weight'], 'L1_gnn_W1': _L1_gnn_in['W1'], 'L1_gnn_W2': _L1_gnn_in['W2'], 'L1_gnn_b1': _L1_gnn_in['b1'], 'L1_gnn_b2': _L1_gnn_in['b2']}

def reference(x, src, dst, edge_type_40, edge_weight, L0_gnn_rFeatures, L0_gnn_relation_weights, L0_gnn_loop_weight, L1_gnn_W1, L1_gnn_W2, L1_gnn_b1, L1_gnn_b2):
    import jax
    import jax.numpy as jnp

    def _L0_gnn_ref(h, rFeatures, relation_weights, loop_weight, norm, edge_src, edge_dst, edge_type):
        import jax, jax.numpy as jnp
        import numpy as np
        N, E, D, R = (6250, 200000, 128, 40)
        DIFFUSION_STEPS = 1
        n, d = h.shape
        r = relation_weights.shape[0]
        seg = edge_dst.astype(jnp.int32) * r + edge_type.astype(jnp.int32)
        for _ in range(DIFFUSION_STEPS):
            S = jax.ops.segment_sum(h[edge_src], seg, num_segments=n * r).reshape(n, r, d)
            cnt = jax.ops.segment_sum(jnp.ones(edge_src.shape, h.dtype), seg, num_segments=n * r).reshape(n, r)
            agg = jnp.einsum('nrd,rdf->nf', S, relation_weights) + cnt @ rFeatures
            h = agg * norm
        h = jax.nn.relu(h + h @ loop_weight)
        return h

    def _L1_gnn_ref(ego_embeddings, W1, W2, b1, b2, adj_vals, src, dst):
        import jax, jax.numpy as jnp
        import numpy as np
        N = 12500
        E = 200000
        D = 128
        NEG_SLOPE = 0.2
        EPS = 1e-12
        msgs = ego_embeddings[src] * adj_vals[:, None]
        lap = jax.ops.segment_sum(msgs, dst, num_segments=ego_embeddings.shape[0])
        first = (ego_embeddings + lap) @ W1 + b1
        second = ego_embeddings * lap @ W2 + b2
        out = jax.nn.leaky_relu(first + second, negative_slope=NEG_SLOPE)
        norm = jnp.sqrt(jnp.sum(out * out, axis=1, keepdims=True))
        return out / jnp.maximum(norm, EPS)
    deg = jnp.maximum(jax.ops.segment_sum(jnp.ones(dst.shape, jnp.float32), dst, num_segments=6250), 1.0)
    deg_isqrt = deg ** (-0.5)
    x = _layernorm(x + _L0_gnn_ref(x, L0_gnn_rFeatures, L0_gnn_relation_weights, L0_gnn_loop_weight, deg_isqrt[:, None], src, dst, edge_type_40), axis=-1)
    x = _layernorm(x + _L1_gnn_ref(x, L1_gnn_W1, L1_gnn_W2, L1_gnn_b1, L1_gnn_b2, edge_weight, src, dst), axis=-1)
    return x

_drawn_inputs = setup_inputs


def setup_inputs(seed=0):
    import zlib

    import numpy as np

    out = dict(_drawn_inputs(seed))
    spreads = {'L1_gnn_b1': (0.0, 2.0), 'L1_gnn_b2': (0.0, 2.0)}
    factors = {'edge_weight': 6.765, 'L1_gnn_W2': 3.057}
    for name, (base, spread) in spreads.items():
        noise = np.random.default_rng([zlib.crc32(name.encode()), seed]).standard_normal(out[name].shape)
        drawn = base * np.exp(spread * noise) if base else spread * noise
        out[name] = jnp.asarray(drawn.astype(out[name].dtype))
    for name, factor in factors.items():
        out[name] = (out[name] * factor).astype(out[name].dtype)
    return out
```

```python
from contextlib import ExitStack

import concourse.bass as bass
from concourse import mybir

ALU = mybir.AluOpType
ACT = mybir.ActivationFunctionType
AX_X = mybir.AxisListType.X
F32 = mybir.dt.float32
I32 = mybir.dt.int32

P = 128
TILE_EDGES = P
GROUP_TILES = 4
GROUP_EDGES = GROUP_TILES * TILE_EDGES
ITER_GROUPS = 4
SLOTS = ITER_GROUPS * GROUP_TILES
WINDOW = 64
LAG = 5
NO_NODE = 1 << 20
LN_EPS = 1e-5
NORM_EPS = 1e-12
SLOPE = 0.2
BANK = 512


def at_least(eng, sem, count):
    if not isinstance(count, int) or count > 0:
        eng.wait_ge(sem, count)


def build(nc, x, src, dst, edge_type, edge_weight, r_features, r_weights, loop_weight,
          w1, w2, b1, b2, out):
    N, D = x.shape
    E = src.shape[0]
    R = r_weights.shape[0]
    assert D == P
    NODE_TILES = -(-N // P)
    LAST_ROWS = N - (NODE_TILES - 1) * P
    NP = NODE_TILES * P
    GROUPS = -(-E // (ITER_GROUPS * GROUP_EDGES)) * ITER_GROUPS
    ITERS = GROUPS // ITER_GROUPS
    GROUP_BLOCKS = -(-GROUPS // P)
    ACC_COLS = NP + WINDOW
    WINDOWS = -(-N // WINDOW)
    CHUNKS = R * D // BANK
    CHUNK_BANKS = 5
    TABLE_COLS = R * D
    assert R * D % BANK == 0 and CHUNKS % (2 * 1) == 0 and CHUNKS % CHUNK_BANKS == 0
    assert GROUPS == -(-E // GROUP_EDGES) and NODE_TILES % 2 == 1 and GROUP_BLOCKS == 2

    table = nc.dram_tensor("message_table", [NP * R, D], F32, kind="Internal").ap()
    x1_rows = nc.dram_tensor("layer0_result", [N, D], F32, kind="Internal").ap()
    table_tiles = table.rearrange("(n r) d -> n (r d)", r=R)

    with ExitStack() as ctx:
        def sb(name, shape, dt=F32):
            return ctx.enter_context(nc.sbuf_tensor(name, shape, dt))

        def sem(name):
            return ctx.enter_context(nc.semaphore(name))

        identity = sb("identity", [P, P])
        ones = sb("ones", [P, P])
        zeros = sb("zeros", [P, P])
        window_iota = sb("window_iota", [P, WINDOW])
        type_iota = sb("type_iota", [P, R])
        group_floor = sb("group_floor", [P, GROUP_BLOCKS])
        relation_w = sb("relation_w", [P, TABLE_COLS])
        r_feat = sb("r_feat", [R, D])
        loop_w = sb("loop_w", [P, D])
        loop_plus_i = sb("loop_plus_i", [P, D])
        w1_sb = sb("w1_sb", [P, D])
        w2_sb = sb("w2_sb", [P, D])
        b1_sb = sb("b1_sb", [1, D])
        b2_sb = sb("b2_sb", [1, D])
        b12_sb = sb("b12_sb", [1, D])
        E_SHAPE = [P, GROUPS, GROUP_TILES]
        e_table_row = sb("e_table_row", E_SHAPE)
        e_src = sb("e_src", E_SHAPE)
        e_type = sb("e_type", E_SHAPE)
        e_local = sb("e_local", E_SHAPE)
        e_dst = sb("e_dst", E_SHAPE)
        e_weight = sb("e_weight", E_SHAPE)
        group_base = sb("group_base", [1, GROUPS], I32)
        stage = sb("stage", [P, 2, TABLE_COLS])
        scratch = stage[:, :, :].rearrange("p s c -> p (s c)")

        def raw(n):
            return scratch[:, n * GROUP_EDGES:(n + 1) * GROUP_EDGES]

        raw_src = [raw(0).bitcast(I32), raw(1).bitcast(I32)]
        raw_dst = [raw(2).bitcast(I32), raw(3).bitcast(I32)]
        raw_type = [raw(4).bitcast(I32), raw(5).bitcast(I32)]
        raw_weight = [raw(6), raw(7)]
        f_src = [raw(8), raw(9)]
        f_dst = [raw(10), raw(11)]
        f_type = [raw(12), raw(13)]
        f_local = [raw(14), raw(15)]
        f_row = [raw(16), raw(17)]
        f_inside = [raw(18), raw(19)]
        span = sb("span", [P, GROUP_BLOCKS, 3])
        span_over = sb("span_over", [P, GROUP_BLOCKS, 3])
        over_row = sb("over_row", [1, GROUP_BLOCKS * 3])
        over_sum = sb("over_sum", [1, 1])
        general = sb("general", [1, 1], I32)

        x_in = sb("x_in", [P, 2, D])
        x_t = sb("x_t", [P, 2, P])
        gathered = sb("gathered", [P, SLOTS, D])
        gather_rows = sb("gather_rows", [P, SLOTS], I32)
        onehot = sb("onehot", [P, ITER_GROUPS, GROUP_TILES, WINDOW])
        type_onehot = sb("type_onehot", [P, ITER_GROUPS, GROUP_TILES, R])
        rel_dst = sb("rel_dst", [P, GROUP_TILES])
        acc = sb("acc", [P, ACC_COLS])
        counts = sb("counts", [R, ACC_COLS])

        node_x = sb("node_x", [P, D])
        count_tile = sb("count_tile", [R, P])
        agg_t = sb("agg_t", [P, P])
        product_t = sb("product_t", [P, P])
        small = sb("small", [P, 16])
        degree, degree_root, degree_norm = small[:, 0:1], small[:, 1:2], small[:, 2:3]
        var_eps, std, rstd = small[:, 3:4], small[:, 4:5], small[:, 5:6]
        square_sum, length, length_floor, inv_length = (
            small[:, 6:7], small[:, 7:8], small[:, 8:9], small[:, 9:10])
        mean_var = small[:, 10:12]
        bn = sb("bn", [P, 6])
        activated = sb("activated", [P, D])
        squares = sb("squares", [P, D])
        residual = sb("residual", [P, D])
        result = sb("result", [P, D])

        psum = ctx.enter_context(nc.psum_tensor("psum", [P, 8, BANK], F32))
        BIAS_BANK, PROJ_BANK = 4, 5
        XT_BANK = CHUNK_BANKS

        weights_in = sem("weights_in")
        edges_in = sem("edges_in")
        base_in = sem("base_in")
        pad_set = sem("pad_set")
        consts_set = sem("consts_set")
        dve_prep = sem("dve_prep")
        floats_ready = sem("floats_ready")
        prep_transposed = sem("prep_transposed")
        prep_stored_act = sem("prep_stored_act")
        prep_stored_dve = sem("prep_stored_dve")
        over_ready = sem("over_ready")
        over_summed = sem("over_summed")
        general_set = sem("general_set")
        x_pad_set = sem("x_pad_set")
        x_loaded = [sem("x_loaded0"), sem("x_loaded1")]
        x_transposed = sem("x_transposed")
        x_t_ready = sem("x_t_ready")
        chunk_ready = sem("chunk_ready")
        chunk_copied_act = sem("chunk_copied_act")
        chunk_copied_dve = sem("chunk_copied_dve")
        table_stored = [sem("table_stored0"), sem("table_stored1")]
        rows_ready = sem("rows_ready")
        gather_done = [sem(f"gather_done{k}") for k in range(SLOTS)]
        onehot_eq = sem("onehot_eq")
        type_onehot_ready = sem("type_onehot_ready")
        onehot_ready = sem("onehot_ready")
        sums_ready = sem("sums_ready")
        acc_added = sem("acc_added")
        sums_added = sem("sums_added")
        gen_rel = sem("gen_rel")
        gen_eq = sem("gen_eq")
        gen_onehot_ready = sem("gen_onehot_ready")
        gen_sum_ready = sem("gen_sum_ready")
        gen_added = sem("gen_added")
        acc_cleared = sem("acc_cleared")
        count_tile_ready = sem("count_tile_ready")
        bias_ready = sem("bias_ready")
        agg_ready = sem("agg_ready")
        degree_ready = sem("degree_ready")
        root_ready = sem("root_ready")
        norm_ready = sem("norm_ready")
        proj_ready = sem("proj_ready")
        activated_ready = sem("activated_ready")
        sloped_ready = sem("sloped_ready")
        leaky_ready = sem("leaky_ready")
        squares_ready = sem("squares_ready")
        length_ready = sem("length_ready")
        length_floored = sem("length_floored")
        inv_length_ready = sem("inv_length_ready")
        node_loaded = sem("node_loaded")
        node_t_ready = sem("node_t_ready")
        residual_ready = sem("residual_ready")
        bn_ready = sem("bn_ready")
        mean_var_ready = sem("mean_var_ready")
        var_eps_ready = sem("var_eps_ready")
        std_ready = sem("std_ready")
        rstd_ready = sem("rstd_ready")
        result_ready = sem("result_ready")
        x1_stored = sem("x1_stored")
        out_stored = sem("out_stored")

        def group_no(layer, i, q):
            return layer * GROUPS + i * ITER_GROUPS + q + 1

        def tile_no(layer, j):
            return layer * NODE_TILES + j + 1

        PREP = [(a, b) for a in range(6) for b in range(GROUP_BLOCKS)]
        prep_in = [f_row, f_src, f_type, f_local, f_dst, raw_weight]
        prep_out = [e_table_row, e_src, e_type, e_local, e_dst, e_weight]

        def fast_or_general(eng, engine, fast, slow):
            eng.wait_ge(general_set, 1)
            flag = engine.value_load(general[0:1, 0:1], min_val=0, max_val=1)
            with eng.If(flag < 1):
                fast()
            with eng.Else():
                slow()

        def run_fast(eng, iteration, node_tile, finish):
            iteration(0)
            with eng.Fori(1, LAG) as i:
                iteration(i)
            iteration(LAG)
            node_tile(0)
            with eng.Fori(LAG + 1, ITERS) as i:
                iteration(i)
                node_tile(i - LAG)
            finish()
            for j in range(ITERS - LAG, NODE_TILES):
                node_tile(j)

        def run_general(eng, iteration, node_tile):
            iteration(0)
            with eng.Fori(1, ITERS) as i:
                iteration(i)
            node_tile(0)
            with eng.Fori(1, NODE_TILES) as j:
                node_tile(j)

        block = ctx.enter_context(nc.Block())

        @block.sync
        def _(sp):
            sp.wait_ge(pad_set, 4)
            FULL = E // GROUP_EDGES
            for b in range(GROUP_BLOCKS):
                g0, g1 = b * P, min((b + 1) * P, FULL)
                for dram, tiles in ((dst, raw_dst), (src, raw_src), (edge_type, raw_type),
                                    (edge_weight, raw_weight)):
                    sp.dma_start(tiles[b][0:g1 - g0, :],
                                 dram[g0 * GROUP_EDGES:g1 * GROUP_EDGES].rearrange(
                                     "(g e) -> g e", e=GROUP_EDGES)).then_inc(edges_in, 16)
            rest = E - FULL * GROUP_EDGES
            for dram, tiles in ((dst, raw_dst), (src, raw_src), (edge_type, raw_type),
                                (edge_weight, raw_weight)):
                sp.dma_start(tiles[-1][FULL % P:FULL % P + 1, 0:rest],
                             dram[FULL * GROUP_EDGES:E].rearrange("(g e) -> g e", g=1)).then_inc(edges_in, 16)
            sp.dma_start(relation_w[:, :].rearrange("p (r f) -> p r f", r=R),
                         r_weights.rearrange("r d f -> d r f")).then_inc(weights_in, 16)
            sp.dma_start(r_feat[:, :], r_features).then_inc(weights_in, 16)
            sp.dma_start(loop_w[:, :], loop_weight).then_inc(weights_in, 16)
            sp.dma_start(w1_sb[:, :], w1).then_inc(weights_in, 16)
            sp.dma_start(w2_sb[:, :], w2).then_inc(weights_in, 16)
            sp.dma_start(b1_sb[:, :], b1).then_inc(weights_in, 16)
            sp.dma_start(b2_sb[:, :], b2).then_inc(weights_in, 16)

            def load_x(t, pair, s):
                if not isinstance(pair, int) or pair > 0:
                    sp.wait_ge(x_transposed, t - 1)
                if isinstance(t, int) and t == NODE_TILES - 1:
                    sp.wait_ge(x_pad_set, 1)
                    sp.dma_start(x_in[0:LAST_ROWS, s, :], x[t * P:N, :]).then_inc(x_loaded[s], 16)
                else:
                    sp.dma_start(x_in[:, s, :], x[bass.ds(t * P, P), :]).then_inc(x_loaded[s], 16)

            def store_table(t, s):
                sp.wait_ge(chunk_copied_act, t * (CHUNKS // 2) + CHUNKS // 2)
                sp.wait_ge(chunk_copied_dve, t * (CHUNKS // 2) + CHUNKS // 2)
                sp.dma_start(table_tiles[bass.ds(t * P, P), :], stage[:, s, :]).then_inc(table_stored[s], 16)

            load_x(0, 0, 0)
            load_x(1, 0, 1)
            with sp.Fori(1, NODE_TILES // 2) as pair:
                for s in range(2):
                    load_x(2 * pair + s, pair, s)
                    store_table(2 * pair - 2 + s, s)
            last = NODE_TILES - 1
            load_x(last, last // 2, 0)
            store_table(last - 2, 0)
            store_table(last - 1, 1)
            store_table(last, 0)

            def node_tile(layer, j):
                at_least(sp, residual_ready, tile_no(layer, j) - 1)
                source = x if layer == 0 else x1_rows
                sink, stored = (x1_rows, x1_stored) if layer == 0 else (out, out_stored)
                if isinstance(j, int) and j == NODE_TILES - 1:
                    rows = slice(j * P, N)
                    n = LAST_ROWS
                else:
                    rows = bass.ds(j * P, P)
                    n = P
                sp.dma_start(node_x[0:n, :], source[rows, :]).then_inc(node_loaded, 16)
                sp.wait_ge(result_ready, tile_no(layer, j))
                sp.dma_start(sink[rows, :], result[0:n, :]).then_inc(stored, 16)

            for layer in range(2):
                if layer == 1:
                    sp.wait_ge(x1_stored, 16 * NODE_TILES)
                node_tile(layer, 0)
                with sp.Fori(1, NODE_TILES - 1) as j:
                    node_tile(layer, j)
                node_tile(layer, NODE_TILES - 1)
            sp.wait_ge(out_stored, 16 * NODE_TILES)

        @block.gpsimd
        def _(pool):
            nc.gpsimd.memset(raw_dst[1], NO_NODE).then_inc(pad_set, 1)
            nc.gpsimd.memset(raw_src[1], 0).then_inc(pad_set, 1)
            nc.gpsimd.memset(raw_type[1], 0).then_inc(pad_set, 1)
            nc.gpsimd.memset(raw_weight[1], 0.0).then_inc(pad_set, 1)
            nc.gpsimd.memset(ones[:, :], 1.0).then_inc(consts_set, 1)
            nc.gpsimd.memset(identity[:, :], 0.0).then_inc(consts_set, 1)
            nc.gpsimd.memset(zeros[:, :], 0.0).then_inc(consts_set, 1)
            nc.gpsimd.iota(window_iota[:, :], pattern=[[1, WINDOW]], base=0, channel_multiplier=0,
                           allow_small_or_imprecise_dtypes=True).then_inc(consts_set, 1)
            nc.gpsimd.iota(type_iota[:, :], pattern=[[1, R]], base=0, channel_multiplier=0,
                           allow_small_or_imprecise_dtypes=True).then_inc(consts_set, 1)
            nc.gpsimd.iota(group_floor[:, :], pattern=[[P // ITER_GROUPS * P, GROUP_BLOCKS]],
                           base=-P * (LAG - 1), channel_multiplier=P // ITER_GROUPS,
                           allow_small_or_imprecise_dtypes=True).then_inc(consts_set, 1)
            pool.wait_ge(consts_set, 6)
            nc.gpsimd.affine_select(out=identity[:, :], in_=identity[:, :], compare_op=ALU.not_equal, fill=1.0,
                                    base=0, pattern=[[-1, P]], channel_multiplier=1).then_inc(consts_set, 1)

            def iteration(layer, i):
                rows = table if layer == 0 else x1_rows
                for h in range(2):
                    pool.wait_ge(rows_ready, 2 * (layer * ITERS + i) + h + 1)
                    pool.nop(nofuse=True)
                    for k in range(h * SLOTS // 2, (h + 1) * SLOTS // 2):
                        nc.gpsimd.indirect_dma_start(
                            gathered[:, k, :], None, rows,
                            bass.IndirectOffsetOnAxis(ap=gather_rows[:, k:k + 1], axis=0),
                        ).then_inc(gather_done[k], 16)

            for layer in range(2):
                if layer == 0:
                    pool.wait_ge(table_stored[0], 16 * (NODE_TILES // 2 + 1))
                    pool.wait_ge(table_stored[1], 16 * (NODE_TILES // 2))
                else:
                    pool.wait_ge(x1_stored, 16 * NODE_TILES)
                with pool.Fori(0, ITERS) as i:
                    iteration(layer, i)

        @block.scalar
        def _(act):
            act.dma_start(group_base[:, :], dst.rearrange("(a n) -> a n", a=1)[:, 0:E:GROUP_EDGES],
                          allow_slow_non_contiguous=True).then_inc(base_in, 16)
            for n, (a, b) in enumerate(PREP):
                if n % 2 == 0:
                    act.wait_ge(prep_transposed, n + 1)
                    g0, g1 = b * P, min((b + 1) * P, GROUPS)
                    nc.scalar.copy(prep_out[a][:, g0:g1, :],
                                   psum[:, n % 8, :].rearrange("p (q g) -> p g q", q=GROUP_TILES)[:, 0:g1 - g0, :]
                                   ).then_inc(prep_stored_act, 1)

            def table_tile(pair, s):
                t = 2 * pair + s
                at_least(act, table_stored[s], 16 * pair)
                for c in range(0, CHUNKS, 2):
                    act.wait_ge(chunk_ready, t * CHUNKS + c + 1)
                    nc.scalar.copy(stage[:, s, c * BANK:(c + 1) * BANK],
                                   psum[:, c % CHUNK_BANKS, :]).then_inc(chunk_copied_act, 1)

            act.wait_ge(prep_stored_dve, len(PREP) // 2)
            for s in range(2):
                table_tile(0, s)
            with act.Fori(1, NODE_TILES // 2) as pair:
                for s in range(2):
                    table_tile(pair, s)
            table_tile(NODE_TILES // 2, 0)

            def iteration(layer, i):
                rows = e_table_row if layer == 0 else e_src
                for h in range(2):
                    at_least(act, sums_ready, group_no(layer, i, 2 * h + 1) - ITER_GROUPS)
                    nc.scalar.copy(gather_rows[:, h * SLOTS // 2:(h + 1) * SLOTS // 2].rearrange(
                        "p (g q) -> p g q", q=GROUP_TILES),
                        rows[:, bass.ds(i * ITER_GROUPS + 2 * h, 2), :]).then_inc(rows_ready, 1)

            def node_tile0(done, j):
                at_least(act, sums_added, done)
                at_least(act, bias_ready, tile_no(0, j) - 1)
                nc.scalar.copy(count_tile[:, :], counts[:, bass.ds(j * P, P)]).then_inc(count_tile_ready, 1)
                act.wait_ge(degree_ready, j + 1)
                nc.scalar.activation(degree_root, degree, ACT.Sqrt).then_inc(root_ready, 1)
                act.wait_ge(norm_ready, j + 1)
                act.wait_ge(proj_ready, tile_no(0, j))
                nc.scalar.activation(activated[:, :], psum[:, PROJ_BANK, 0:D], ACT.Relu,
                                     scale=degree_norm).then_inc(activated_ready, 1)
                act.wait_ge(var_eps_ready, tile_no(0, j))
                nc.scalar.activation(std, var_eps, ACT.Sqrt).then_inc(std_ready, 1)

            def node_tile1(j):
                act.wait_ge(proj_ready, tile_no(1, j))
                at_least(act, leaky_ready, j)
                nc.scalar.mul(squares[:, :], psum[:, PROJ_BANK, 0:D], SLOPE).then_inc(sloped_ready, 1)
                act.wait_ge(leaky_ready, j + 1)
                nc.scalar.activation(squares[:, :], activated[:, :], ACT.Square,
                                     accum_out=square_sum).then_inc(squares_ready, 1)
                act.wait_ge(squares_ready, j + 1)
                nc.scalar.activation(length, square_sum, ACT.Sqrt).then_inc(length_ready, 1)
                act.wait_ge(var_eps_ready, tile_no(1, j))
                nc.scalar.activation(std, var_eps, ACT.Sqrt).then_inc(std_ready, 1)

            for layer in range(2):
                node_tile = (lambda j: node_tile0(0, j)) if layer == 0 else node_tile1

                def fast(layer=layer):
                    def tile(j):
                        if layer == 0:
                            node_tile0((j + LAG) * ITER_GROUPS if not isinstance(j, int)
                                       else min(j + LAG, ITERS) * ITER_GROUPS, j)
                        else:
                            node_tile1(j)
                    run_fast(act, lambda i: iteration(layer, i), tile, lambda: None)

                def slow(layer=layer):
                    def tile(j):
                        if layer == 0:
                            node_tile0(GROUPS, j)
                        else:
                            node_tile1(j)
                    run_general(act, lambda i: iteration(layer, i), tile)

                fast_or_general(act, nc.scalar, fast, slow)

        @block.vector
        def _(dve):
            steps = [0]

            def step(ins):
                steps[0] += 1
                ins.then_inc(dve_prep, 1)
                dve.wait_ge(dve_prep, steps[0])

            nc.vector.memset(counts[:, :], 0.0).then_inc(acc_cleared, 1)
            nc.vector.memset(acc[:, :], 0.0).then_inc(acc_cleared, 1)
            dve.wait_ge(edges_in, 16 * 4 * (GROUP_BLOCKS + 1))
            for b in range(GROUP_BLOCKS):
                nc.vector.tensor_copy(f_dst[b], raw_dst[b])
                nc.vector.tensor_copy(f_src[b], raw_src[b])
                ins = nc.vector.tensor_copy(f_type[b], raw_type[b])
            step(ins)
            for b in range(GROUP_BLOCKS):
                nc.vector.tensor_scalar(f_local[b], f_dst[b], f_dst[b][:, 0:1], None, ALU.subtract)
                ins = nc.vector.scalar_tensor_tensor(f_row[b], f_src[b], float(R), f_type[b], ALU.mult, ALU.add)
            ins.then_inc(floats_ready, 1)
            dve.wait_ge(floats_ready, 1)
            dve.wait_ge(consts_set, 7)
            for b in range(GROUP_BLOCKS):
                nc.vector.scalar_tensor_tensor(f_inside[b], f_local[b], float(NO_NODE // 2), f_local[b],
                                               ALU.is_lt, ALU.mult)
                nc.vector.tensor_reduce(span[:, b, 0:1], f_local[b], AX_X, ALU.min)
                ins = nc.vector.tensor_tensor(span[:, b, 2:3], group_floor[:, b:b + 1], f_dst[b][:, 0:1],
                                              ALU.subtract)
            step(ins)
            for b in range(GROUP_BLOCKS):
                ins = nc.vector.tensor_reduce(span[:, b, 1:2], f_inside[b], AX_X, ALU.max)
            step(ins)
            for b in range(GROUP_BLOCKS):
                nc.vector.tensor_scalar(span_over[:, b, 0:1], span[:, b, 0:1], 0.0, None, ALU.is_lt)
                nc.vector.tensor_scalar(span_over[:, b, 1:2], span[:, b, 1:2], float(WINDOW), None, ALU.is_ge)
                ins = nc.vector.tensor_scalar(span_over[:, b, 2:3], span[:, b, 2:3], 0.0, None, ALU.is_gt)
            step(ins)
            ins.then_inc(over_ready, 1) if False else None
            nc.vector.tensor_copy(small[:, 0:1], span_over[:, 0, 0:1]).then_inc(over_ready, 1)
            for n, (a, b) in enumerate(PREP):
                if n % 2 == 1:
                    dve.wait_ge(prep_transposed, n + 1)
                    g0, g1 = b * P, min((b + 1) * P, GROUPS)
                    nc.vector.tensor_copy(prep_out[a][:, g0:g1, :],
                                          psum[:, n % 8, :].rearrange("p (q g) -> p g q", q=GROUP_TILES)[:, 0:g1 - g0, :]
                                          ).then_inc(prep_stored_dve, 1)
            dve.wait_ge(over_summed, 1)
            step(nc.vector.tensor_reduce(over_sum[:, :], psum[0:1, XT_BANK, 0:GROUP_BLOCKS * 3], AX_X, ALU.add))
            nc.vector.tensor_scalar(general[:, :], over_sum[:, :], 0.5, None, ALU.is_gt).then_inc(general_set, 1)
            dve.wait_ge(weights_in, 16 * 7)
            step(nc.vector.tensor_tensor(loop_plus_i[:, :], loop_w[:, :], identity[:, :], ALU.add))
            step(nc.vector.tensor_tensor(b12_sb[:, :], b1_sb[:, :], b2_sb[:, :], ALU.add))
            step(nc.vector.memset(node_x[:, :], 0.0))
            dve.wait_ge(prep_stored_act, len(PREP) // 2)
            step(nc.vector.memset(result[:, :], 0.0))

            def table_tile(pair, s):
                t = 2 * pair + s
                dve.wait_ge(x_transposed, t + 1)
                at_least(dve, chunk_ready, (t - 1) * CHUNKS)
                nc.vector.tensor_copy(x_t[:, s, :], psum[:, XT_BANK + s, 0:P]).then_inc(x_t_ready, 1)
                at_least(dve, table_stored[s], 16 * pair)
                for c in range(1, CHUNKS, 2):
                    dve.wait_ge(chunk_ready, t * CHUNKS + c + 1)
                    nc.vector.tensor_copy(stage[:, s, c * BANK:(c + 1) * BANK],
                                          psum[:, c % CHUNK_BANKS, :]).then_inc(chunk_copied_dve, 1)

            for s in range(2):
                table_tile(0, s)
            with dve.Fori(1, NODE_TILES // 2 - 1) as pair:
                for s in range(2):
                    table_tile(pair, s)
            table_tile(NODE_TILES // 2 - 1, 0)
            nc.vector.memset(x_in[:, 0, :], 0.0).then_inc(x_pad_set, 1)
            table_tile(NODE_TILES // 2 - 1, 1)
            table_tile(NODE_TILES // 2, 0)

            dve.wait_ge(acc_cleared, 2)
            dve.wait_ge(base_in, 16)

            def make_onehots(layer, i, q, first):
                g = i * ITER_GROUPS + q
                at_least(dve, sums_ready, group_no(layer, i, q) - ITER_GROUPS)
                local = e_local[:, bass.ds(g, 1), :].rearrange("p a q -> p (a q)")
                hot = onehot[:, q, :, :]
                if layer == 0:
                    kind = e_type[:, bass.ds(g, 1), :].rearrange("p a q -> p (a q)")
                    nc.vector.tensor_tensor(
                        type_onehot[:, q, :, :], type_iota[:, None, :].to_broadcast([P, GROUP_TILES, R]),
                        kind[:, :, None].to_broadcast([P, GROUP_TILES, R]), ALU.is_equal
                    ).then_inc(type_onehot_ready, 1)
                eq = nc.vector.tensor_tensor(
                    hot, window_iota[:, None, :].to_broadcast([P, GROUP_TILES, WINDOW]),
                    local[:, :, None].to_broadcast([P, GROUP_TILES, WINDOW]), ALU.is_equal)
                if layer == 0:
                    eq.then_inc(onehot_ready, 1)
                else:
                    eq.then_inc(onehot_eq, 1)
                    weight = e_weight[:, bass.ds(g, 1), :].rearrange("p a q -> p (a q)")
                    dve.wait_ge(onehot_eq, g + 1)
                    nc.vector.tensor_tensor(hot, hot, weight[:, :, None].to_broadcast([P, GROUP_TILES, WINDOW]),
                                            ALU.mult).then_inc(onehot_ready, 1)

            def add_sums(layer, i, q):
                g = i * ITER_GROUPS + q
                base = nc.vector.value_load(group_base[0:1, bass.ds(g, 1)], min_val=0, max_val=N - 1)
                dve.wait_ge(sums_ready, group_no(layer, i, q))
                at_least(dve, sums_added, group_no(layer, i, q) - 1)
                if layer == 0:
                    near = counts[:, bass.ds(base, WINDOW)]
                    nc.vector.tensor_tensor(near, near, psum[0:R, q, WINDOW:2 * WINDOW],
                                            ALU.add).then_inc(acc_added, 1)
                near = acc[:, bass.ds(base, WINDOW)]
                nc.vector.tensor_tensor(near, near, psum[:, q, 0:WINDOW], ALU.add).then_inc(sums_added, 1)

            def iteration(layer, i):
                for q in range(ITER_GROUPS):
                    make_onehots(layer, i, q, False)
                    if not isinstance(i, int) or i > 0:
                        add_sums(layer, i - 1, q)

            def general_iteration(layer, i):
                for q in range(ITER_GROUPS):
                    g = i * ITER_GROUPS + q
                    if layer == 0:
                        kind = e_type[:, bass.ds(g, 1), :].rearrange("p a q -> p (a q)")
                        nc.vector.tensor_tensor(
                            type_onehot[:, 0, :, :], type_iota[:, None, :].to_broadcast([P, GROUP_TILES, R]),
                            kind[:, :, None].to_broadcast([P, GROUP_TILES, R]), ALU.is_equal
                        ).then_inc(type_onehot_ready, 1)

                    def window(w):
                        n = (layer * GROUPS + g) * WINDOWS + w
                        where = e_dst[:, bass.ds(g, 1), :].rearrange("p a q -> p (a q)")
                        if isinstance(w, int) and w == 0:
                            nc.vector.tensor_copy(rel_dst[:, :], where).then_inc(gen_rel, 1)
                        else:
                            nc.vector.tensor_scalar(rel_dst[:, :], rel_dst[:, :], -float(WINDOW), None,
                                                    ALU.add).then_inc(gen_rel, 1)
                        dve.wait_ge(gen_rel, n + 1)
                        hot = onehot[:, 0, :, :]
                        nc.vector.tensor_tensor(
                            hot, window_iota[:, None, :].to_broadcast([P, GROUP_TILES, WINDOW]),
                            rel_dst[:, :, None].to_broadcast([P, GROUP_TILES, WINDOW]), ALU.is_equal
                        ).then_inc(gen_eq, 1)
                        dve.wait_ge(gen_eq, n + 1)
                        if layer == 0:
                            nc.vector.tensor_scalar(rel_dst[:, :], rel_dst[:, :], 0.0, None,
                                                    ALU.add).then_inc(gen_onehot_ready, 1)
                        else:
                            weight = e_weight[:, bass.ds(g, 1), :].rearrange("p a q -> p (a q)")
                            nc.vector.tensor_tensor(hot, hot,
                                                    weight[:, :, None].to_broadcast([P, GROUP_TILES, WINDOW]),
                                                    ALU.mult).then_inc(gen_onehot_ready, 1)
                        dve.wait_ge(gen_sum_ready, n + 1)
                        if layer == 0:
                            near = counts[:, bass.ds(w * WINDOW, WINDOW)]
                            nc.vector.tensor_tensor(near, near, psum[0:R, 0, WINDOW:2 * WINDOW], ALU.add)
                        near = acc[:, bass.ds(w * WINDOW, WINDOW)]
                        nc.vector.tensor_tensor(near, near, psum[:, 0, 0:WINDOW], ALU.add).then_inc(gen_added, 1)
                        dve.wait_ge(gen_added, n + 1)
                        dve.nop(nofuse=True)

                    window(0)
                    with dve.Fori(1, WINDOWS - 1) as w:
                        window(w)
                    window(WINDOWS - 1)
                    nc.vector.tensor_copy(rel_dst[:, :], where_of(g)).then_inc(sums_added, 1)
                    dve.wait_ge(sums_added, group_no(layer, i, q))

            def where_of(g):
                return e_dst[:, bass.ds(g, 1), :].rearrange("p a q -> p (a q)")

            def layer_norm(layer, j, stored):
                n = tile_no(layer, j)
                dve.wait_ge(residual_ready, n)
                nc.vector.bn_stats(bn[:, :], residual[:, :]).then_inc(bn_ready, 1)
                dve.wait_ge(bn_ready, n)
                dve.nop(nofuse=True)
                nc.vector.bn_aggr(mean_var, bn[:, :]).then_inc(mean_var_ready, 1)
                dve.wait_ge(mean_var_ready, n)
                nc.vector.tensor_scalar(var_eps, mean_var[:, 1:2], LN_EPS, None, ALU.add).then_inc(var_eps_ready, 1)
                dve.wait_ge(std_ready, n)
                nc.vector.reciprocal(rstd, std).then_inc(rstd_ready, 1)
                dve.wait_ge(rstd_ready, n)
                at_least(dve, stored, 16 * j)
                nc.vector.tensor_scalar(result[:, :], residual[:, :], mean_var[:, 0:1], rstd,
                                        ALU.subtract, ALU.mult).then_inc(result_ready, 1)

            def node_tile0(j):
                n = tile_no(0, j)
                cols = acc[:, bass.ds(j * P, P)]
                dve.wait_ge(bias_ready, n)
                at_least(dve, proj_ready, n - 1)
                nc.vector.tensor_tensor(agg_t[:, :], cols, psum[:, BIAS_BANK, 0:P], ALU.add).then_inc(agg_ready, 1)
                nc.vector.tensor_scalar(degree, psum[:, BIAS_BANK, P:P + 1], 1.0, None,
                                        ALU.max).then_inc(degree_ready, 1)
                dve.wait_ge(agg_ready, n)
                dve.nop(nofuse=True)
                nc.vector.tensor_copy(cols, zeros[:, :])
                dve.wait_ge(root_ready, j + 1)
                nc.vector.reciprocal(degree_norm, degree_root).then_inc(norm_ready, 1)
                dve.wait_ge(activated_ready, n)
                dve.wait_ge(node_loaded, 16 * n)
                nc.vector.tensor_tensor(residual[:, :], activated[:, :], node_x[:, :],
                                        ALU.add).then_inc(residual_ready, 1)
                layer_norm(0, j, x1_stored)

            def node_tile1(j):
                n = tile_no(1, j)
                cols = acc[:, bass.ds(j * P, P)]
                dve.wait_ge(node_t_ready, j + 1)
                at_least(dve, proj_ready, n - 1)
                nc.vector.tensor_tensor(agg_t[:, :], cols, psum[:, BIAS_BANK, 0:P], ALU.add)
                nc.vector.tensor_tensor(product_t[:, :], cols, psum[:, BIAS_BANK, 0:P],
                                        ALU.mult).then_inc(agg_ready, 1)
                dve.wait_ge(sloped_ready, j + 1)
                nc.vector.tensor_tensor(activated[:, :], psum[:, PROJ_BANK, 0:D], squares[:, :],
                                        ALU.max).then_inc(leaky_ready, 1)
                dve.wait_ge(length_ready, j + 1)
                nc.vector.tensor_scalar(length_floor, length, NORM_EPS, None, ALU.max).then_inc(length_floored, 1)
                dve.wait_ge(length_floored, j + 1)
                nc.vector.reciprocal(inv_length, length_floor).then_inc(inv_length_ready, 1)
                dve.wait_ge(inv_length_ready, j + 1)
                nc.vector.scalar_tensor_tensor(residual[:, :], activated[:, :], inv_length, node_x[:, :],
                                               ALU.mult, ALU.add).then_inc(residual_ready, 1)
                layer_norm(1, j, out_stored)

            for layer in range(2):
                node_tile = node_tile0 if layer == 0 else node_tile1

                def fast(layer=layer, node_tile=node_tile):
                    def finish():
                        for q in range(ITER_GROUPS):
                            add_sums(layer, ITERS - 1, q)
                        dve.wait_ge(sums_added, (layer + 1) * GROUPS)

                    run_fast(dve, lambda i: iteration(layer, i), node_tile, finish)

                def slow(layer=layer, node_tile=node_tile):
                    run_general(dve, lambda i: general_iteration(layer, i), node_tile)

                fast_or_general(dve, nc.vector, fast, slow)

        @block.tensor
        def _(pe):
            pe.wait_ge(consts_set, 7)
            pe.wait_ge(floats_ready, 1)
            for n, (a, b) in enumerate(PREP):
                at_least(pe, prep_stored_dve if n % 2 else prep_stored_act, (n - 8) // 2 + 1)
                for q in range(GROUP_TILES):
                    ins = nc.tensor.transpose(psum[:, n % 8, q * P:(q + 1) * P],
                                              prep_in[a][b][:, q * P:(q + 1) * P], identity[:, :])
                ins.then_inc(prep_transposed, 1)
            pe.wait_ge(over_ready, 1)
            pe.wait_ge(prep_stored_act, len(PREP) // 2)
            pe.wait_ge(prep_stored_dve, len(PREP) // 2)
            nc.tensor.matmul(psum[0:1, XT_BANK, 0:GROUP_BLOCKS * 3], ones[:, 0:1],
                             span_over[:, :, :].rearrange("p b s -> p (b s)"), start=True, stop=True
                             ).then_inc(over_summed, 1)
            pe.wait_ge(weights_in, 16 * 7)
            pe.wait_ge(general_set, 1)

            def transpose_x(t, pair, s):
                pe.wait_ge(x_loaded[s], 16 * (pair + 1))
                nc.tensor.transpose(psum[:, XT_BANK + s, 0:P], x_in[:, s, :], identity[:, :]
                                    ).then_inc(x_transposed, 1)

            def table_tile(t, pair, s):
                pe.wait_ge(x_t_ready, t + 1)
                for c in range(CHUNKS):
                    past = c - CHUNK_BANKS
                    if not isinstance(t, int) or t * CHUNKS + past >= 0:
                        if past % 2 == 0:
                            pe.wait_ge(chunk_copied_act, t * (CHUNKS // 2) + past // 2 + 1)
                        else:
                            pe.wait_ge(chunk_copied_dve, t * (CHUNKS // 2) + past // 2 + 1)
                    nc.tensor.matmul(psum[:, c % CHUNK_BANKS, :], x_t[:, s, :],
                                     relation_w[:, c * BANK:(c + 1) * BANK], start=True, stop=True
                                     ).then_inc(chunk_ready, 1)

            transpose_x(0, 0, 0)
            transpose_x(1, 0, 1)
            table_tile(0, 0, 0)
            with pe.Fori(1, NODE_TILES // 2) as pair:
                transpose_x(2 * pair, pair, 0)
                table_tile(2 * pair - 1, pair - 1, 1)
                transpose_x(2 * pair + 1, pair, 1)
                table_tile(2 * pair, pair, 0)
            last = NODE_TILES - 1
            transpose_x(last, last // 2, 0)
            table_tile(last - 1, last // 2 - 1, 1)
            table_tile(last, last // 2, 0)

            def group_sums(layer, k0, hot, kinds, bank, slots_ready):
                for k in range(GROUP_TILES):
                    slots_ready(k0 + k)
                    ins = nc.tensor.matmul(psum[:, bank, 0:WINDOW], gathered[:, k0 + k, :], hot[:, k, :],
                                           start=(k == 0), stop=(k == GROUP_TILES - 1))
                if layer == 0:
                    for k in range(GROUP_TILES):
                        ins = nc.tensor.matmul(psum[0:R, bank, WINDOW:2 * WINDOW], kinds[:, k, :], hot[:, k, :],
                                               start=(k == 0), stop=(k == GROUP_TILES - 1))
                return ins

            def iteration(layer, i):
                for q in range(ITER_GROUPS):
                    pe.wait_ge(onehot_ready, group_no(layer, i, q))
                    at_least(pe, sums_added, group_no(layer, i, q) - ITER_GROUPS)
                    group_sums(layer, q * GROUP_TILES, onehot[:, q, :, :], type_onehot[:, q, :, :], q,
                               lambda k: pe.wait_ge(gather_done[k], 16 * (layer * ITERS + i + 1))
                               ).then_inc(sums_ready, 1)

            def general_iteration(layer, i):
                for q in range(ITER_GROUPS):
                    g = i * ITER_GROUPS + q
                    for k in range(q * GROUP_TILES, (q + 1) * GROUP_TILES):
                        pe.wait_ge(gather_done[k], 16 * (layer * ITERS + i + 1))

                    def window(w):
                        n = (layer * GROUPS + g) * WINDOWS + w
                        pe.wait_ge(gen_onehot_ready, n + 1)
                        at_least(pe, gen_added, n)
                        return group_sums(layer, q * GROUP_TILES, onehot[:, 0, :, :], type_onehot[:, 0, :, :],
                                          0, lambda k: None).then_inc(gen_sum_ready, 1)

                    window(0)
                    with pe.Fori(1, WINDOWS - 1) as w:
                        window(w)
                    window(WINDOWS - 1)
                    nc.tensor.matmul(psum[:, 1, 0:WINDOW], gathered[:, q * GROUP_TILES, :], onehot[:, 0, 0, :],
                                     start=True, stop=True).then_inc(sums_ready, 1)

            def node_tile0(j):
                n = tile_no(0, j)
                pe.wait_ge(count_tile_ready, j + 1)
                at_least(pe, degree_ready, j)
                nc.tensor.matmul(psum[:, BIAS_BANK, 0:P], r_feat[:, :], count_tile[:, :], start=True, stop=True)
                nc.tensor.matmul(psum[:, BIAS_BANK, P:P + 1], count_tile[:, :], ones[0:R, 0:1],
                                 start=True, stop=True).then_inc(bias_ready, 1)
                pe.wait_ge(agg_ready, n)
                at_least(pe, activated_ready, n - 1)
                nc.tensor.matmul(psum[:, PROJ_BANK, 0:D], agg_t[:, :], loop_plus_i[:, :],
                                 start=True, stop=True).then_inc(proj_ready, 1)

            def node_tile1(j):
                n = tile_no(1, j)
                pe.wait_ge(node_loaded, 16 * n)
                pe.wait_ge(agg_ready, n - 1)
                nc.tensor.transpose(psum[:, BIAS_BANK, 0:P], node_x[:, :], identity[:, :]).then_inc(node_t_ready, 1)
                pe.wait_ge(agg_ready, n)
                pe.wait_ge(activated_ready, NODE_TILES)
                at_least(pe, leaky_ready, j)
                nc.tensor.matmul(psum[:, PROJ_BANK, 0:D], agg_t[:, :], w1_sb[:, :], start=True, stop=False)
                nc.tensor.matmul(psum[:, PROJ_BANK, 0:D], product_t[:, :], w2_sb[:, :], start=False, stop=False)
                nc.tensor.matmul(psum[:, PROJ_BANK, 0:D], ones[0:1, :], b12_sb[:, :],
                                 start=False, stop=True).then_inc(proj_ready, 1)

            for layer in range(2):
                node_tile = node_tile0 if layer == 0 else node_tile1

                def fast(layer=layer, node_tile=node_tile):
                    run_fast_tiles_first(layer, node_tile)

                def slow(layer=layer, node_tile=node_tile):
                    run_general(pe, lambda i: general_iteration(layer, i), node_tile)

                def run_fast_tiles_first(layer, node_tile):
                    iteration(layer, 0)
                    with pe.Fori(1, LAG) as i:
                        iteration(layer, i)
                    node_tile(0)
                    iteration(layer, LAG)
                    with pe.Fori(LAG + 1, ITERS) as i:
                        node_tile(i - LAG)
                        iteration(layer, i)
                    for j in range(ITERS - LAG, NODE_TILES):
                        node_tile(j)

                fast_or_general(pe, nc.tensor, fast, slow)


_INS = ["x", "src", "dst", "edge_type_40", "edge_weight", "L0_gnn_rFeatures", "L0_gnn_relation_weights",
        "L0_gnn_loop_weight", "L1_gnn_W1", "L1_gnn_W2", "L1_gnn_b1", "L1_gnn_b2"]


def kernel(**inputs):
    import numpy as _np
    import concourse.bacc as _bacc
    from concourse import mybir as _mybir
    from concourse.bass_utils import run_bass_kernel_spmd as _run

    nc = _bacc.Bacc("TRN2", target_bir_lowering=False, num_devices=1)
    arrays, args = {}, []
    for name in _INS:
        a = _np.ascontiguousarray(inputs[name])
        arrays[f"in_{name}_dram"] = a
        args.append(nc.dram_tensor(f"in_{name}_dram", a.shape, _mybir.dt.from_np(a.dtype), kind="ExternalInput").ap())
    shape = inputs["x"].shape
    args.append(nc.dram_tensor("out_dram", shape, _mybir.dt.float32, kind="ExternalOutput").ap())
    build(nc, *args)
    r = _run(nc, [arrays], core_ids=[0])
    return r.results[0]["out_dram"]
```

```python
from contextlib import ExitStack

import concourse.bass as bass
from concourse import mybir

ALU = mybir.AluOpType
ACT = mybir.ActivationFunctionType
AX_X = mybir.AxisListType.X
F32 = mybir.dt.float32
F32R = mybir.dt.float32r
BF16 = mybir.dt.bfloat16
I32 = mybir.dt.int32

P = 128
TILE_EDGES = P
GROUP_TILES = 4
GROUP_EDGES = GROUP_TILES * TILE_EDGES
ITER_GROUPS = 4
SLOTS = ITER_GROUPS * GROUP_TILES
WINDOW = 64
TILE_WINDOW = 12
ITER_WINDOW = 136
LAGS = (6, 5)
ADD_LAG = 8
ACT_ONEHOTS = (1, 3, 5, 7, 9, 11, 13, 15)
RELATIONS_BEHIND = {2: 3, 3: 3, 4: 4, 5: 3, 6: 3, 7: 4, 8: 3, 9: 3, 10: 4, 11: 3, 12: 3, 13: 4}
CLEAR_PARTS = 4
CLEARS = {0: 0, 2: 1, 4: 2, 6: 3}
SPLIT_TILES = 7
NO_TYPE = 1 << 10
NO_NODE = 1 << 20
LN_EPS = 1e-5
NORM_EPS = 1e-12
SLOPE = 0.2
BANK = 512


def at_least(eng, sem, count):
    if not isinstance(count, int) or count > 0:
        eng.wait_ge(sem, count)


def build(nc, x, src, dst, edge_type, edge_weight, r_features, r_weights, loop_weight,
          w1, w2, b1, b2, out):
    N, D = x.shape
    E = src.shape[0]
    R = r_weights.shape[0]
    assert D == P
    NODE_TILES = -(-N // P)
    LAST_ROWS = N - (NODE_TILES - 1) * P
    NP = NODE_TILES * P
    GROUPS = -(-E // (ITER_GROUPS * GROUP_EDGES)) * ITER_GROUPS
    ITERS = GROUPS // ITER_GROUPS
    GROUP_BLOCKS = -(-GROUPS // P)
    ACC_COLS = NP + ITER_WINDOW
    TILES = ITERS * SLOTS
    JOINT = R * TILE_WINDOW
    S_COLS = R * ITER_WINDOW
    DVE_ONEHOTS = tuple(k for k in range(SLOTS) if k not in ACT_ONEHOTS)
    WINDOWS = -(-N // WINDOW)
    CHUNKS = R * D // BANK
    CHUNK_RELATIONS = BANK // D
    assert JOINT <= BANK and sum(RELATIONS_BEHIND.values()) == R and R % CLEAR_PARTS == 0
    assert GROUPS == -(-E // GROUP_EDGES) and GROUP_BLOCKS == 2 and NODE_TILES % SPLIT_TILES == 0

    x_split = nc.dram_tensor("x_split", [N, 2 * D], F32, kind="Internal").ap()
    x1_rows = nc.dram_tensor("layer0_result", [N, D], F32, kind="Internal").ap()

    SPANS = 5

    with ExitStack() as ctx:
        def sb(name, shape, dt=F32):
            return ctx.enter_context(nc.sbuf_tensor(name, shape, dt))

        def sem(name):
            return ctx.enter_context(nc.semaphore(name))

        identity = sb("identity", [P, P])
        ones = sb("ones", [P, P])
        zeros = sb("zeros", [P, P])
        zeros_wide = sb("zeros_wide", [P, S_COLS // 20])
        window_iota = sb("window_iota", [P, WINDOW])
        type_iota = sb("type_iota", [P, R])
        group_floor = sb("group_floor", [P, GROUP_BLOCKS])
        joint_iota = sb("joint_iota", [P, JOINT])
        relation_w = sb("relation_w", [P, R * D])
        r_feat = sb("r_feat", [R, D])
        loop_w = sb("loop_w", [P, D])
        loop_plus_i = sb("loop_plus_i", [P, D])
        w1_sb = sb("w1_sb", [P, D])
        w2_sb = sb("w2_sb", [P, D])
        b1_sb = sb("b1_sb", [1, D])
        b2_sb = sb("b2_sb", [1, D])
        b12_sb = sb("b12_sb", [1, D])
        E_SHAPE = [P, GROUPS, GROUP_TILES]
        e_joint = sb("e_joint", E_SHAPE)
        e_src = sb("e_src", E_SHAPE)
        e_type = sb("e_type", E_SHAPE)
        e_local = sb("e_local", E_SHAPE)
        e_dst = sb("e_dst", E_SHAPE)
        e_weight = sb("e_weight", E_SHAPE)
        group_base = sb("group_base", [1, GROUPS], I32)
        tile_base = sb("tile_base", [1, ITERS, SLOTS], I32)
        tile_base_f = sb("tile_base_f", [1, ITERS, SLOTS])
        tile_offset_f = sb("tile_offset_f", [1, ITERS, SLOTS])
        tile_offset = sb("tile_offset", [1, ITERS, SLOTS], I32)
        offset_span = sb("offset_span", [1, 2])
        offset_over = sb("offset_over", [1, 2])
        sums = sb("sums", [P, 2, S_COLS])
        scratch = sums[:, :, :].rearrange("p s c -> p (s c)")

        def raw(n):
            return scratch[:, n * GROUP_EDGES:(n + 1) * GROUP_EDGES]

        raw_src = [raw(0).bitcast(I32), raw(1).bitcast(I32)]
        raw_dst = [raw(2).bitcast(I32), raw(3).bitcast(I32)]
        raw_type = [raw(4).bitcast(I32), raw(5).bitcast(I32)]
        raw_weight = [raw(6), raw(7)]
        f_src = [raw(8), raw(9)]
        f_dst = [raw(10), raw(11)]
        f_type = [raw(12), raw(13)]
        f_local = [raw(14), raw(15)]
        f_joint = [raw(16), raw(17)]
        f_inside = [raw(18), raw(19)]
        f_tile_local = [raw(2), raw(3)]
        span = sb("span", [P, GROUP_BLOCKS, SPANS])
        span_over = sb("span_over", [P, GROUP_BLOCKS, SPANS])
        over_sum = sb("over_sum", [1, 3])
        general = sb("general", [1, 1], I32)

        gathered_parts = sb("gathered_parts", [P, SLOTS, 2, D], F32R)
        gathered = sb("gathered", [P, SLOTS, D])
        x_in = gathered[:, 0:SPLIT_TILES, :]
        x_parts = gathered_parts[:, 0:SPLIT_TILES, :, :]
        joint_onehot = sb("joint_onehot", [P, ADD_LAG, JOINT], F32R)
        distance = sb("distance", [P, JOINT])
        gather_rows = sb("gather_rows", [P, SLOTS], I32)
        onehot = sb("onehot", [P, ITER_GROUPS, GROUP_TILES, WINDOW])
        dst_onehot = sb("dst_onehot", [P, ITER_GROUPS, GROUP_TILES, WINDOW], BF16)
        type_onehot = sb("type_onehot", [P, ITER_GROUPS, GROUP_TILES, R], BF16)
        rel_dst = sb("rel_dst", [P, GROUP_TILES])
        acc = sb("acc", [P, ACC_COLS])
        counts = sb("counts", [R, ACC_COLS])

        node_x = sb("node_x", [P, D])
        count_tile = sb("count_tile", [R, P])
        agg_t = sb("agg_t", [P, P])
        product_t = sb("product_t", [P, P])
        type_mask = sb("type_mask", [P, R])
        small = sb("small", [P, 16])
        degree, degree_root, degree_norm = small[:, 0:1], small[:, 1:2], small[:, 2:3]
        var_eps, std, rstd = small[:, 3:4], small[:, 4:5], small[:, 5:6]
        square_sum, length, length_floor, inv_length = (
            small[:, 6:7], small[:, 7:8], small[:, 8:9], small[:, 9:10])
        mean_var = small[:, 10:12]
        bn = sb("bn", [P, 6])
        activated = sb("activated", [P, D])
        squares = sb("squares", [P, D])
        residual = sb("residual", [P, D])
        result = sb("result", [P, D])

        psum = ctx.enter_context(nc.psum_tensor("psum", [P, 8, BANK], F32))
        RING = 4
        SUM_BANK, NODE_BANK, COUNT_BANKS = 4, 6, (5, 7)
        node_bias = psum[:, NODE_BANK, 0:P]
        node_degree = psum[:, NODE_BANK, P:P + 1]
        node_proj = psum[:, NODE_BANK, 2 * P:3 * P]

        def count_sums(q):
            return psum[0:R, COUNT_BANKS[q % 2], 0:WINDOW]

        weights_in = sem("weights_in")
        edges_in = sem("edges_in")
        base_in = sem("base_in")
        pad_set = sem("pad_set")
        consts_set = sem("consts_set")
        dve_prep = sem("dve_prep")
        floats_ready = sem("floats_ready")
        prep_transposed = sem("prep_transposed")
        prep_stored_act = sem("prep_stored_act")
        prep_stored_dve = sem("prep_stored_dve")
        over_ready = sem("over_ready")
        over_summed = sem("over_summed")
        general_set = sem("general_set")
        x_loaded = sem("x_loaded")
        x_high_ready = sem("x_high_ready")
        x_low_ready = sem("x_low_ready")
        parts_stored = sem("parts_stored")
        joint_ready_dve = sem("joint_ready_dve")
        joint_ready_act = sem("joint_ready_act")
        distance_ready = sem("distance_ready")
        tile_sums_ready = sem("tile_sums_ready")
        tile_added = sem("tile_added")
        sums_cleared = sem("sums_cleared")
        iter_products_part = sem("iter_products_part")
        mask_ready = sem("mask_ready")
        message_step = sem("message_step")
        iter_added = sem("iter_added")
        counts_ready = sem("counts_ready")
        counts_added = sem("counts_added")
        offsets_set = sem("offsets_set")
        parts_summed = sem("parts_summed")
        message_x_t = sem("message_x_t")
        message_x_t_ready = sem("message_x_t_ready")
        products_ready = sem("products_ready")
        rows_ready = sem("rows_ready")
        gather_done = [sem(f"gather_done{k}") for k in range(SLOTS)]
        onehot_eq = sem("onehot_eq")
        type_onehot_ready = sem("type_onehot_ready")
        onehot_ready = sem("onehot_ready")
        sums_ready = sem("sums_ready")
        acc_added = sem("acc_added")
        sums_added = sem("sums_added")
        gen_rel = sem("gen_rel")
        gen_eq = sem("gen_eq")
        gen_onehot_ready = sem("gen_onehot_ready")
        gen_sum_ready = sem("gen_sum_ready")
        gen_added = sem("gen_added")
        acc_cleared = sem("acc_cleared")
        count_tile_ready = sem("count_tile_ready")
        bias_ready = sem("bias_ready")
        agg_ready = sem("agg_ready")
        degree_ready = sem("degree_ready")
        root_ready = sem("root_ready")
        norm_ready = sem("norm_ready")
        proj_ready = sem("proj_ready")
        activated_ready = sem("activated_ready")
        sloped_ready = sem("sloped_ready")
        leaky_ready = sem("leaky_ready")
        squares_ready = sem("squares_ready")
        length_ready = sem("length_ready")
        length_floored = sem("length_floored")
        inv_length_ready = sem("inv_length_ready")
        node_loaded = sem("node_loaded")
        node_t_ready = sem("node_t_ready")
        residual_ready = sem("residual_ready")
        bn_ready = sem("bn_ready")
        mean_var_ready = sem("mean_var_ready")
        var_eps_ready = sem("var_eps_ready")
        std_ready = sem("std_ready")
        rstd_ready = sem("rstd_ready")
        result_ready = sem("result_ready")
        x1_stored = sem("x1_stored")
        out_stored = sem("out_stored")

        def group_no(layer, i, q):
            return layer * GROUPS + i * ITER_GROUPS + q + 1

        def tile_no(layer, j):
            return layer * NODE_TILES + j + 1

        PREP = [(a, b) for a in range(6) for b in range(GROUP_BLOCKS)]
        prep_in = [f_joint, f_src, f_type, f_local, f_dst, raw_weight]
        prep_out = [e_joint, e_src, e_type, e_local, e_dst, e_weight]

        def fast_or_general(eng, engine, fast, slow):
            eng.wait_ge(general_set, 1)
            flag = engine.value_load(general[0:1, 0:1], min_val=0, max_val=1)
            with eng.If(flag < 1):
                fast()
            with eng.Else():
                slow()

        def tile_count(i, k):
            return i * SLOTS + k + 1

        def run_fast(eng, lag, iteration, node_tile, finish, tile_first=False):
            def both(i):
                if tile_first:
                    node_tile(i - lag)
                iteration(i)
                if not tile_first:
                    node_tile(i - lag)

            iteration(0)
            with eng.Fori(1, lag) as i:
                iteration(i)
            both(lag)
            with eng.Fori(lag + 1, ITERS) as i:
                both(i)
            finish()
            for j in range(ITERS - lag, NODE_TILES):
                node_tile(j)

        def run_fast_pairs(eng, lag, iteration, node_tile, finish):
            def pair(p, with_tiles):
                for s in range(2):
                    i = 2 * p + s
                    has_last = with_tiles and not (isinstance(i, int) and i == lag)
                    iteration(i, s, i - lag if with_tiles else None, i - lag - 1 if has_last else None)

            pair(0, False)
            with eng.Fori(1, lag // 2) as p:
                pair(p, False)
            pair(lag // 2, True)
            with eng.Fori(lag // 2 + 1, ITERS // 2) as p:
                pair(p, True)
            finish()
            for j in range(ITERS - lag, NODE_TILES):
                node_tile(j)

        def run_general(eng, iteration, node_tile):
            iteration(0)
            with eng.Fori(1, ITERS) as i:
                iteration(i)
            node_tile(0)
            with eng.Fori(1, NODE_TILES) as j:
                node_tile(j)

        block = ctx.enter_context(nc.Block())

        @block.sync
        def _(sp):
            def load_edges():
                FULL = E // GROUP_EDGES
                for b in range(GROUP_BLOCKS):
                    g0, g1 = b * P, min((b + 1) * P, FULL)
                    for dram, tiles in ((dst, raw_dst), (src, raw_src), (edge_type, raw_type),
                                        (edge_weight, raw_weight)):
                        sp.dma_start(tiles[b][0:g1 - g0, :],
                                     dram[g0 * GROUP_EDGES:g1 * GROUP_EDGES].rearrange(
                                         "(g e) -> g e", e=GROUP_EDGES)).then_inc(edges_in, 16)
                rest = E - FULL * GROUP_EDGES
                for dram, tiles in ((dst, raw_dst), (src, raw_src), (edge_type, raw_type),
                                    (edge_weight, raw_weight)):
                    sp.dma_start(tiles[-1][FULL % P:FULL % P + 1, 0:rest],
                                 dram[FULL * GROUP_EDGES:E].rearrange("(g e) -> g e", g=1)).then_inc(edges_in, 16)
                sp.dma_start(relation_w[:, :].rearrange("p (r f) -> p r f", r=R),
                             r_weights.rearrange("r d f -> d r f")).then_inc(weights_in, 16)
                sp.dma_start(r_feat[:, :], r_features).then_inc(weights_in, 16)
                sp.dma_start(loop_w[:, :], loop_weight).then_inc(weights_in, 16)
                sp.dma_start(w1_sb[:, :], w1).then_inc(weights_in, 16)
                sp.dma_start(w2_sb[:, :], w2).then_inc(weights_in, 16)
                sp.dma_start(b1_sb[:, :], b1).then_inc(weights_in, 16)
                sp.dma_start(b2_sb[:, :], b2).then_inc(weights_in, 16)

            for step in range(NODE_TILES // SPLIT_TILES):
                if step == 1:
                    sp.wait_ge(pad_set, 5)
                    load_edges()
                t0 = step * SPLIT_TILES
                at_least(sp, x_high_ready, step)
                at_least(sp, x_low_ready, step)
                full = min(SPLIT_TILES, N // P - t0)
                sp.dma_start(x_in[:, 0:full, :],
                             x[t0 * P:(t0 + full) * P, :].rearrange("(t p) d -> p t d", p=P)).then_inc(x_loaded, 16)
                if full < SPLIT_TILES:
                    sp.dma_start(x_in[0:LAST_ROWS, full, :], x[(t0 + full) * P:N, :]).then_inc(x_loaded, 16)
                sp.wait_ge(x_high_ready, step + 1)
                sp.wait_ge(x_low_ready, step + 1)
                sp.dma_start(x_split[t0 * P:(t0 + full) * P, :].rearrange("(t p) d -> p t d", p=P),
                             x_parts[:, 0:full, :, :].rearrange("p t a d -> p t (a d)").bitcast(F32)).then_inc(parts_stored, 16)
                if full < SPLIT_TILES:
                    sp.dma_start(x_split[(t0 + full) * P:N, :],
                                 x_parts[0:LAST_ROWS, full, :, :].rearrange("p a d -> p (a d)").bitcast(F32)
                                 ).then_inc(parts_stored, 16)
            def node_tile(layer, j):
                at_least(sp, residual_ready, tile_no(layer, j) - 1)
                source = x if layer == 0 else x1_rows
                sink, stored = (x1_rows, x1_stored) if layer == 0 else (out, out_stored)
                if isinstance(j, int) and j == NODE_TILES - 1:
                    rows = slice(j * P, N)
                    n = LAST_ROWS
                else:
                    rows = bass.ds(j * P, P)
                    n = P
                sp.dma_start(node_x[0:n, :], source[rows, :]).then_inc(node_loaded, 16)
                sp.wait_ge(result_ready, tile_no(layer, j))
                sp.dma_start(sink[rows, :], result[0:n, :]).then_inc(stored, 16)

            for layer in range(2):
                if layer == 1:
                    sp.wait_ge(x1_stored, 16 * NODE_TILES)
                node_tile(layer, 0)
                with sp.Fori(1, NODE_TILES - 1) as j:
                    node_tile(layer, j)
                node_tile(layer, NODE_TILES - 1)
            sp.wait_ge(out_stored, 16 * NODE_TILES)

        @block.gpsimd
        def _(pool):
            nc.gpsimd.memset(raw_dst[1], NO_NODE).then_inc(pad_set, 1)
            nc.gpsimd.memset(raw_src[1], 0).then_inc(pad_set, 1)
            nc.gpsimd.memset(raw_type[1], NO_TYPE).then_inc(pad_set, 1)
            nc.gpsimd.memset(raw_weight[1], 0.0).then_inc(pad_set, 1)
            nc.gpsimd.memset(tile_base[:, :, :], 0).then_inc(pad_set, 1)
            nc.gpsimd.memset(ones[:, :], 1.0).then_inc(consts_set, 1)
            nc.gpsimd.memset(identity[:, :], 0.0).then_inc(consts_set, 1)
            nc.gpsimd.memset(zeros[:, :], 0.0).then_inc(consts_set, 1)
            nc.gpsimd.iota(window_iota[:, :], pattern=[[1, WINDOW]], base=0, channel_multiplier=0,
                           allow_small_or_imprecise_dtypes=True).then_inc(consts_set, 1)
            nc.gpsimd.iota(type_iota[:, :], pattern=[[1, R]], base=0, channel_multiplier=0,
                           allow_small_or_imprecise_dtypes=True).then_inc(consts_set, 1)
            nc.gpsimd.iota(joint_iota[:, :], pattern=[[1, JOINT]], base=0, channel_multiplier=0,
                           allow_small_or_imprecise_dtypes=True).then_inc(consts_set, 1)
            nc.gpsimd.iota(group_floor[:, :], pattern=[[P // ITER_GROUPS * P, GROUP_BLOCKS]],
                           base=-P * (LAGS[1] - 1), channel_multiplier=P // ITER_GROUPS,
                           allow_small_or_imprecise_dtypes=True).then_inc(consts_set, 1)
            pool.wait_ge(consts_set, 7)
            nc.gpsimd.affine_select(out=identity[:, :], in_=identity[:, :], compare_op=ALU.not_equal, fill=1.0,
                                    base=0, pattern=[[-1, P]], channel_multiplier=1).then_inc(consts_set, 1)

            def iteration(layer, i):
                rows, slots = (x_split, gathered_parts[:, :, :, :].rearrange("p s a d -> p s (a d)").bitcast(F32)
                               ) if layer == 0 else (x1_rows, gathered[:, :, :])
                for h in range(2):
                    pool.wait_ge(rows_ready, 2 * (layer * ITERS + i) + h + 1)
                    pool.nop(nofuse=True)
                    for k in range(h * SLOTS // 2, (h + 1) * SLOTS // 2):
                        nc.gpsimd.indirect_dma_start(
                            slots[:, k, :], None, rows,
                            bass.IndirectOffsetOnAxis(ap=gather_rows[:, k:k + 1], axis=0),
                        ).then_inc(gather_done[k], 16)

            for layer in range(2):
                if layer == 0:
                    pool.wait_ge(parts_stored, 16 * (NODE_TILES // SPLIT_TILES + 1))
                else:
                    pool.wait_ge(x1_stored, 16 * NODE_TILES)
                with pool.Fori(0, ITERS) as i:
                    iteration(layer, i)

        @block.scalar
        def _(act):
            FIRSTS = -(-E // TILE_EDGES)
            act.wait_ge(pad_set, 5)
            act.dma_start(tile_base[:, :, :].rearrange("a i k -> a (i k)")[:, 0:FIRSTS],
                          dst.rearrange("(a n) -> a n", a=1)[:, 0:E:TILE_EDGES],
                          allow_slow_non_contiguous=True).then_inc(base_in, 16)

            for step in range(NODE_TILES // SPLIT_TILES):
                at_least(act, parts_stored, 16 * step)
                act.wait_ge(x_loaded, 16 * (step + 1 + (step == NODE_TILES // SPLIT_TILES - 1)))
                nc.scalar.copy(x_parts[:, :, 0, :], x_in[:, :, :]).then_inc(x_high_ready, 1)

            for n, (a, b) in enumerate(PREP):
                if n % 2 == 0:
                    act.wait_ge(prep_transposed, n + 1)
                    g0, g1 = b * P, min((b + 1) * P, GROUPS)
                    nc.scalar.copy(prep_out[a][:, g0:g1, :],
                                   psum[:, n % 8, :].rearrange("p (q g) -> p g q", q=GROUP_TILES)[:, 0:g1 - g0, :]
                                   ).then_inc(prep_stored_act, 1)

            act.wait_ge(prep_stored_dve, len(PREP) // 2)
            act.wait_ge(acc_cleared, 3)

            def write_rows(layer, i, h):
                if layer == 0:
                    at_least(act, tile_sums_ready, tile_count(i, (h + 1) * SLOTS // 2 - 1) - SLOTS)
                else:
                    at_least(act, tile_sums_ready, TILES)
                    at_least(act, sums_ready, group_no(0, i, 2 * h + 1) - ITER_GROUPS)
                nc.scalar.copy(gather_rows[:, h * SLOTS // 2:(h + 1) * SLOTS // 2].rearrange(
                    "p (g q) -> p g q", q=GROUP_TILES),
                    e_src[:, bass.ds(i * ITER_GROUPS + 2 * h, 2), :]).then_inc(rows_ready, 1)

            def iteration0(i, s, j, last_j):
                for k in range(SLOTS):
                    if k == 0:
                        write_rows(0, i, 0)
                        if j is not None:
                            copy_counts((i - 1) * ITER_GROUPS, j)
                    if k in CLEARS:
                        part = CLEARS[k]
                        at_least(act, iter_products_part, CLEAR_PARTS * (i - 2) + part + 1)
                        cols = sums[:, s, part * S_COLS // CLEAR_PARTS:(part + 1) * S_COLS // CLEAR_PARTS]
                        nc.scalar.mul(cols.rearrange("p (a c) -> p a c", c=S_COLS // 20),
                                      zeros_wide[:, None, :].to_broadcast([P, 20 // CLEAR_PARTS, S_COLS // 20]),
                                      1.0).then_inc(sums_cleared, 1)
                    if k in ACT_ONEHOTS:
                        n = i * len(ACT_ONEHOTS) + ACT_ONEHOTS.index(k) + 1
                        at_least(act, joint_ready_act, n - 1)
                        key = e_joint[:, :, :].rearrange("p g q -> p (g q)")[:, bass.ds(i * SLOTS + k, 1)]
                        nc.scalar.activation(distance[:, :], joint_iota[:, :], ACT.Abs, bias=key,
                                             scale=-1.0).then_inc(distance_ready, 1)
                        act.wait_ge(distance_ready, n)
                        at_least(act, tile_sums_ready, tile_count(i, k) - ADD_LAG)
                        nc.scalar.activation(joint_onehot[:, k % ADD_LAG, :], distance[:, :], ACT.Relu,
                                             bias=1.0, scale=-1.0).then_inc(joint_ready_act, 1)
                    if k == SLOTS // 2 - 1:
                        write_rows(0, i, 1)
                    if last_j is not None and k == 8:
                        norm_sqrt(0, last_j)
                    if j is not None and k == 11:
                        degree_sqrt(j)
                    if j is not None and k == 15:
                        project_relu(j)

            def iteration(layer, i):
                for h in range(2):
                    write_rows(layer, i, h)

            def copy_counts(done, j):
                at_least(act, counts_added, done)
                at_least(act, bias_ready, j)
                nc.scalar.copy(count_tile[:, :], counts[:, bass.ds(j * P, P)]).then_inc(count_tile_ready, 1)

            def degree_sqrt(j):
                act.wait_ge(degree_ready, j + 1)
                nc.scalar.activation(degree_root, degree, ACT.Sqrt).then_inc(root_ready, 1)

            def project_relu(j):
                act.wait_ge(norm_ready, j + 1)
                act.wait_ge(proj_ready, j + 1)
                nc.scalar.activation(activated[:, :], node_proj, ACT.Relu,
                                     scale=degree_norm).then_inc(activated_ready, 1)

            def norm_sqrt(layer, j):
                act.wait_ge(var_eps_ready, tile_no(layer, j))
                nc.scalar.activation(std, var_eps, ACT.Sqrt).then_inc(std_ready, 1)

            def node_tile0(j):
                copy_counts(GROUPS, j)
                degree_sqrt(j)
                project_relu(j)
                norm_sqrt(0, j)

            def node_tile1(j):
                act.wait_ge(proj_ready, tile_no(1, j))
                at_least(act, leaky_ready, j)
                nc.scalar.mul(squares[:, :], node_proj, SLOPE).then_inc(sloped_ready, 1)
                act.wait_ge(leaky_ready, j + 1)
                nc.scalar.activation(squares[:, :], activated[:, :], ACT.Square,
                                     accum_out=square_sum).then_inc(squares_ready, 1)
                act.wait_ge(squares_ready, j + 1)
                nc.scalar.activation(length, square_sum, ACT.Sqrt).then_inc(length_ready, 1)
                norm_sqrt(1, j)

            fast_or_general(act, nc.scalar,
                            lambda: run_fast_pairs(act, LAGS[0], iteration0, node_tile0,
                                                   lambda: norm_sqrt(0, ITERS - 1 - LAGS[0])),
                            lambda: run_general(act, lambda i: iteration(0, i), node_tile0))
            fast_or_general(act, nc.scalar,
                            lambda: run_fast(act, LAGS[1], lambda i: iteration(1, i), node_tile1, lambda: None),
                            lambda: run_general(act, lambda i: iteration(1, i), node_tile1))

        @block.vector
        def _(dve):
            steps = [0]

            def step(ins):
                steps[0] += 1
                ins.then_inc(dve_prep, 1)
                dve.wait_ge(dve_prep, steps[0])


            def split(step):
                dve.wait_ge(x_high_ready, step + 1)
                nc.vector.tensor_tensor(x_parts[:, :, 1, :], x_in[:, :, :], x_parts[:, :, 0, :].bitcast(F32),
                                        ALU.subtract).then_inc(x_low_ready, 1)

            for n in range(NODE_TILES // SPLIT_TILES):
                split(n)
            nc.vector.memset(zeros_wide[:, :], 0.0).then_inc(acc_cleared, 1)
            nc.vector.memset(counts[:, :], 0.0).then_inc(acc_cleared, 1)
            nc.vector.memset(acc[:, :], 0.0).then_inc(acc_cleared, 1)
            dve.wait_ge(edges_in, 16 * 4 * (GROUP_BLOCKS + 1))
            for b in range(GROUP_BLOCKS):
                nc.vector.tensor_copy(f_dst[b], raw_dst[b])
                nc.vector.tensor_copy(f_src[b], raw_src[b])
                ins = nc.vector.tensor_copy(f_type[b], raw_type[b])
            step(ins)
            for b in range(GROUP_BLOCKS):
                nc.vector.tensor_scalar(f_local[b], f_dst[b], f_dst[b][:, 0:1], None, ALU.subtract)
                for q in range(GROUP_TILES):
                    tile = slice(q * P, (q + 1) * P)
                    ins = nc.vector.tensor_scalar(f_tile_local[b][:, tile], f_dst[b][:, tile],
                                                  f_dst[b][:, q * P:q * P + 1], None, ALU.subtract)
            step(ins)
            for b in range(GROUP_BLOCKS):
                ins = nc.vector.scalar_tensor_tensor(f_joint[b], f_type[b], float(TILE_WINDOW), f_tile_local[b],
                                                     ALU.mult, ALU.add)
            ins.then_inc(floats_ready, 1)
            dve.wait_ge(floats_ready, 1)
            dve.wait_ge(consts_set, 8)
            for b in range(GROUP_BLOCKS):
                nc.vector.scalar_tensor_tensor(f_inside[b], f_local[b], float(NO_NODE // 2), f_local[b],
                                               ALU.is_lt, ALU.mult)
                nc.vector.tensor_reduce(span[:, b, 0:1], f_local[b], AX_X, ALU.min)
                nc.vector.tensor_reduce(span[:, b, 3:4], f_tile_local[b], AX_X, ALU.min)
                ins = nc.vector.tensor_tensor(span[:, b, 2:3], group_floor[:, b:b + 1], f_dst[b][:, 0:1],
                                              ALU.subtract)
            step(ins)
            for b in range(GROUP_BLOCKS):
                ins = nc.vector.tensor_reduce(span[:, b, 1:2], f_inside[b], AX_X, ALU.max)
            step(ins)
            for b in range(GROUP_BLOCKS):
                ins = nc.vector.scalar_tensor_tensor(f_inside[b], f_tile_local[b], float(NO_NODE // 2),
                                                     f_tile_local[b], ALU.is_lt, ALU.mult)
            step(ins)
            for b in range(GROUP_BLOCKS):
                ins = nc.vector.tensor_reduce(span[:, b, 4:5], f_inside[b], AX_X, ALU.max)
            step(ins)
            for b in range(GROUP_BLOCKS):
                for n, (bound, op) in enumerate(((0.0, ALU.is_lt), (float(WINDOW), ALU.is_ge), (0.0, ALU.is_gt),
                                                 (0.0, ALU.is_lt), (float(TILE_WINDOW), ALU.is_ge))):
                    ins = nc.vector.tensor_scalar(span_over[:, b, n:n + 1], span[:, b, n:n + 1], bound, None, op)
            ins.then_inc(over_ready, 1)
            dve.wait_ge(base_in, 16)
            step(nc.vector.tensor_copy(tile_base_f[:, :, :], tile_base[:, :, :]))
            step(nc.vector.tensor_tensor(tile_offset_f[:, :, :], tile_base_f[:, :, :],
                                         tile_base_f[:, :, 0:1].to_broadcast([1, ITERS, SLOTS]), ALU.subtract))
            nc.vector.tensor_scalar(group_base[:, :], tile_base_f[:, :, :].rearrange("a i k -> a (i k)")[
                :, 0:TILES:GROUP_TILES], 0.0, float(N - 1), ALU.max, ALU.min)
            PAD_TILES = TILES - -(-E // TILE_EDGES)
            step(nc.vector.memset(tile_offset_f[:, ITERS - 1, SLOTS - PAD_TILES:SLOTS], 0.0))
            nc.vector.tensor_reduce(offset_span[:, 0:1], tile_offset_f[:, :, :].rearrange("a i k -> a (i k)"),
                                    AX_X, ALU.min)
            step(nc.vector.tensor_reduce(offset_span[:, 1:2], tile_offset_f[:, :, :].rearrange("a i k -> a (i k)"),
                                         AX_X, ALU.max))
            nc.vector.tensor_scalar(offset_over[:, 0:1], offset_span[:, 0:1], 0.0, None, ALU.is_lt)
            nc.vector.tensor_scalar(offset_over[:, 1:2], offset_span[:, 1:2], float(ITER_WINDOW - TILE_WINDOW),
                                    None, ALU.is_gt)
            nc.vector.tensor_scalar(tile_offset[:, :, :], tile_offset_f[:, :, :], 0.0,
                                    float(ITER_WINDOW - TILE_WINDOW), ALU.max, ALU.min).then_inc(offsets_set, 1)
            for n, (a, b) in enumerate(PREP):
                if n % 2 == 1:
                    dve.wait_ge(prep_transposed, n + 1)
                    g0, g1 = b * P, min((b + 1) * P, GROUPS)
                    nc.vector.tensor_copy(prep_out[a][:, g0:g1, :],
                                          psum[:, n % 8, :].rearrange("p (q g) -> p g q", q=GROUP_TILES)[:, 0:g1 - g0, :]
                                          ).then_inc(prep_stored_dve, 1)
            dve.wait_ge(over_summed, 1)
            dve.wait_ge(offsets_set, 1)
            step(nc.vector.tensor_reduce(over_sum[:, 0:1], psum[0:1, SUM_BANK, 0:GROUP_BLOCKS * SPANS], AX_X,
                                         ALU.add))
            step(nc.vector.tensor_tensor(over_sum[:, 1:2], over_sum[:, 0:1], offset_over[:, 0:1], ALU.add))
            step(nc.vector.tensor_tensor(over_sum[:, 2:3], over_sum[:, 1:2], offset_over[:, 1:2], ALU.add))
            nc.vector.tensor_scalar(general[:, :], over_sum[:, 2:3], 0.5, None, ALU.is_gt).then_inc(general_set, 1)
            dve.wait_ge(weights_in, 16 * 7)
            step(nc.vector.tensor_tensor(loop_plus_i[:, :], loop_w[:, :], identity[:, :], ALU.add))
            step(nc.vector.tensor_tensor(b12_sb[:, :], b1_sb[:, :], b2_sb[:, :], ALU.add))
            dve.wait_ge(prep_stored_act, len(PREP) // 2)

            dve.wait_ge(acc_cleared, 3)

            def make_type_onehot(g, q):
                kind = e_type[:, bass.ds(g, 1), :].rearrange("p a q -> p (a q)")
                nc.vector.tensor_tensor(
                    type_onehot[:, q, :, :], type_iota[:, None, :].to_broadcast([P, GROUP_TILES, R]),
                    kind[:, :, None].to_broadcast([P, GROUP_TILES, R]), ALU.is_equal
                ).then_inc(type_onehot_ready, 1)

            def make_dst_onehot(g, hot):
                local = e_local[:, bass.ds(g, 1), :].rearrange("p a q -> p (a q)")
                return nc.vector.tensor_tensor(
                    hot, window_iota[:, None, :].to_broadcast([P, GROUP_TILES, WINDOW]),
                    local[:, :, None].to_broadcast([P, GROUP_TILES, WINDOW]), ALU.is_equal)

            def make_weighted_onehot(i, q):
                g = i * ITER_GROUPS + q
                hot = onehot[:, q, :, :]
                at_least(dve, sums_ready, group_no(0, i, q) - ITER_GROUPS)
                make_dst_onehot(g, hot).then_inc(onehot_eq, 1)
                weight = e_weight[:, bass.ds(g, 1), :].rearrange("p a q -> p (a q)")
                dve.wait_ge(onehot_eq, g + 1)
                nc.vector.tensor_tensor(hot, hot, weight[:, :, None].to_broadcast([P, GROUP_TILES, WINDOW]),
                                        ALU.mult).then_inc(onehot_ready, 1)

            def load_base(g):
                return nc.values_load_multi_w_load_instructions(
                    group_base[0:1, bass.ds(g, 1)], engines=(mybir.EngineType.DVE,), min_val=0, max_val=N - 1,
                    skip_runtime_bounds_check_because="group_base is clamped to these bounds")[1][0]

            def add_counts(i, q):
                g = i * ITER_GROUPS + q
                base = load_base(g)
                dve.wait_ge(counts_ready, g + 1)
                at_least(dve, counts_added, g)
                near = counts[:, bass.ds(base, WINDOW)]
                nc.vector.tensor_tensor(near, near, count_sums(q),
                                        ALU.add).then_inc(counts_added, 1)

            def add_sums(i, q):
                g = i * ITER_GROUPS + q
                base = load_base(g)
                dve.wait_ge(sums_ready, g + 1)
                at_least(dve, sums_added, g)
                near = acc[:, bass.ds(base, WINDOW)]
                nc.vector.tensor_tensor(near, near, psum[:, q, 0:WINDOW], ALU.add).then_inc(sums_added, 1)

            def iteration(i):
                for q in range(ITER_GROUPS):
                    make_weighted_onehot(i, q)
                    if not isinstance(i, int) or i > 0:
                        add_sums(i - 1, q)

            def load_offsets(i, half):
                row = tile_offset[0:1, bass.ds(i, 1), half * SLOTS // 2:(half + 1) * SLOTS // 2]
                return nc.values_load_multi_w_load_instructions(row.rearrange("a i k -> a (i k)"), engines=(mybir.EngineType.DVE,),
                                            min_val=0, max_val=ITER_WINDOW - TILE_WINDOW,
                    skip_runtime_bounds_check_because="tile_offset is clamped to these bounds")[1]

            def add_tile(i, s, k, offset):
                n = tile_count(i, k)
                dve.wait_ge(tile_sums_ready, n)
                if k == 0:
                    dve.wait_ge(sums_cleared, CLEAR_PARTS * (i + 1))
                at_least(dve, tile_added, n - 1)
                near = sums[:, s, :].rearrange("p (r n) -> p r n", r=R)[:, :, bass.ds(offset, TILE_WINDOW)]
                tile_sums = psum[:, k % RING, 0:JOINT].rearrange("p (r n) -> p r n", r=R)
                nc.vector.tensor_tensor(near, near, tile_sums, ALU.add).then_inc(tile_added, 1)

            def add_iteration(i):
                base = load_base(i * ITER_GROUPS)
                dve.wait_ge(iter_products_part, CLEAR_PARTS * (i + 1))
                at_least(dve, iter_added, i)
                near = acc[:, bass.ds(base, ITER_WINDOW)]
                nc.vector.tensor_tensor(near, near, psum[:, SUM_BANK, 0:ITER_WINDOW],
                                        ALU.add).then_inc(iter_added, 1)

            def iteration0(i, s, j, last_j):
                first = isinstance(i, int) and i == 0
                offsets = None if first else load_offsets(i - 1, 1)
                for k in range(SLOTS):
                    q = k // GROUP_TILES
                    g = i * ITER_GROUPS + q
                    if k == ADD_LAG:
                        offsets = load_offsets(i, 0)
                    if k in DVE_ONEHOTS:
                        at_least(dve, tile_sums_ready, tile_count(i, k) - ADD_LAG)
                        key = e_joint[:, :, :].rearrange("p g q -> p (g q)")[:, bass.ds(i * SLOTS + k, 1)]
                        nc.vector.tensor_scalar(joint_onehot[:, k % ADD_LAG, :], joint_iota[:, :], key, None,
                                                ALU.is_equal).then_inc(joint_ready_dve, 1)
                    if k % GROUP_TILES == 1:
                        at_least(dve, counts_ready, group_no(0, i, q) - ITER_GROUPS)
                        make_type_onehot(g, q)
                    if k % GROUP_TILES == 3:
                        make_dst_onehot(g, dst_onehot[:, q, :, :]).then_inc(onehot_ready, 1)
                    if k == 10 and j is not None:
                        take_bias(j)
                    if k == 13 and j is not None:
                        degree_reciprocal(j)
                    if last_j is not None:
                        if k == 1:
                            add_residual(last_j)
                        if k in NORM_STEPS:
                            NORM_STEPS[k](0, last_j)
                    if k >= ADD_LAG:
                        add_tile(i, s, k - ADD_LAG, offsets[k - ADD_LAG])
                    elif not first:
                        add_tile(i - 1, 1 - s, k + SLOTS - ADD_LAG, offsets[k])
                    if k == 5 and (not isinstance(i, int) or i >= 2):
                        add_iteration(i - 2)
                    if k % GROUP_TILES == 3:
                        if q >= 2:
                            add_counts(i, q - 2)
                        elif not first:
                            add_counts(i - 1, q + 2)

            def finish0():
                last = ITERS - 1
                offsets = load_offsets(last, 1)
                last_j = last - LAGS[0]
                for k in range(ADD_LAG):
                    add_tile(last, 1, k + SLOTS - ADD_LAG, offsets[k])
                    if k == 1:
                        add_residual(last_j)
                        layer_norm(0, last_j)
                for q in range(2, ITER_GROUPS):
                    add_counts(last, q)
                add_iteration(last - 1)
                add_iteration(last)
                dve.wait_ge(iter_added, ITERS)

            def make_messages(g, q):
                for k in range(GROUP_TILES):
                    n = g * GROUP_TILES + k
                    slot = q * GROUP_TILES + k
                    dve.wait_ge(gather_done[slot], 16 * rounds(g, q))
                    nc.vector.tensor_tensor(residual[:, :], gathered_parts[:, slot, 0, :].bitcast(F32),
                                            gathered_parts[:, slot, 1, :].bitcast(F32),
                                            ALU.add).then_inc(parts_summed, 1)
                    dve.wait_ge(message_x_t, n + 1)
                    nc.vector.tensor_copy(agg_t[:, :], node_bias).then_inc(message_x_t_ready, 1)
                    message = gathered[:, slot, :]
                    for r in range(R):
                        if r % CHUNK_RELATIONS == 0:
                            dve.wait_ge(products_ready, n * CHUNKS + r // CHUNK_RELATIONS + 1)
                        mask = type_mask[:, r:r + 1]
                        if r == 0:
                            kind = e_type[:, bass.ds(g, 1), k:k + 1].rearrange("p a q -> p (a q)")
                            nc.vector.tensor_scalar(type_mask[:, :], type_iota[:, :], kind, None,
                                                    ALU.is_equal).then_inc(mask_ready, 1)
                            dve.wait_ge(mask_ready, n + 1)
                        product = psum[:, r // CHUNK_RELATIONS % 2, r % CHUNK_RELATIONS * D:
                                       (r % CHUNK_RELATIONS + 1) * D]
                        if r == 0:
                            ins = nc.vector.tensor_scalar(message, product, mask, None, ALU.mult)
                        else:
                            dve.wait_ge(message_step, n * R + r)
                            ins = nc.vector.scalar_tensor_tensor(message, product, mask, message,
                                                                 ALU.mult, ALU.add)
                        ins.then_inc(message_step, 1)
                dve.wait_ge(message_step, (g + 1) * GROUP_TILES * R)
                dve.nop(nofuse=True)

            def rounds(g, q):
                return this_iteration[0] + 1

            this_iteration = [0]

            def general_iteration(layer, i):
                this_iteration[0] = i
                for q in range(ITER_GROUPS):
                    g = i * ITER_GROUPS + q
                    if layer == 0:
                        make_messages(g, q)
                        kind = e_type[:, bass.ds(g, 1), :].rearrange("p a q -> p (a q)")
                        nc.vector.tensor_tensor(
                            type_onehot[:, 0, :, :], type_iota[:, None, :].to_broadcast([P, GROUP_TILES, R]),
                            kind[:, :, None].to_broadcast([P, GROUP_TILES, R]), ALU.is_equal
                        ).then_inc(type_onehot_ready, 1)

                    def window(w):
                        n = (layer * GROUPS + g) * WINDOWS + w
                        where = e_dst[:, bass.ds(g, 1), :].rearrange("p a q -> p (a q)")
                        if isinstance(w, int) and w == 0:
                            nc.vector.tensor_copy(rel_dst[:, :], where).then_inc(gen_rel, 1)
                        else:
                            nc.vector.tensor_scalar(rel_dst[:, :], rel_dst[:, :], -float(WINDOW), None,
                                                    ALU.add).then_inc(gen_rel, 1)
                        dve.wait_ge(gen_rel, n + 1)
                        hot = onehot[:, 0, :, :]
                        if layer == 0:
                            nc.vector.tensor_tensor(
                                dst_onehot[:, 0, :, :],
                                window_iota[:, None, :].to_broadcast([P, GROUP_TILES, WINDOW]),
                                rel_dst[:, :, None].to_broadcast([P, GROUP_TILES, WINDOW]), ALU.is_equal)
                        nc.vector.tensor_tensor(
                            hot, window_iota[:, None, :].to_broadcast([P, GROUP_TILES, WINDOW]),
                            rel_dst[:, :, None].to_broadcast([P, GROUP_TILES, WINDOW]), ALU.is_equal
                        ).then_inc(gen_eq, 1)
                        dve.wait_ge(gen_eq, n + 1)
                        if layer == 0:
                            nc.vector.tensor_scalar(rel_dst[:, :], rel_dst[:, :], 0.0, None,
                                                    ALU.add).then_inc(gen_onehot_ready, 1)
                        else:
                            weight = e_weight[:, bass.ds(g, 1), :].rearrange("p a q -> p (a q)")
                            nc.vector.tensor_tensor(hot, hot,
                                                    weight[:, :, None].to_broadcast([P, GROUP_TILES, WINDOW]),
                                                    ALU.mult).then_inc(gen_onehot_ready, 1)
                        dve.wait_ge(gen_sum_ready, n + 1)
                        if layer == 0:
                            near = counts[:, bass.ds(w * WINDOW, WINDOW)]
                            nc.vector.tensor_tensor(near, near, count_sums(0), ALU.add)
                        near = acc[:, bass.ds(w * WINDOW, WINDOW)]
                        nc.vector.tensor_tensor(near, near, psum[:, 0, 0:WINDOW], ALU.add).then_inc(gen_added, 1)
                        dve.wait_ge(gen_added, n + 1)
                        dve.nop(nofuse=True)

                    window(0)
                    with dve.Fori(1, WINDOWS - 1) as w:
                        window(w)
                    window(WINDOWS - 1)
                    dve.wait_ge(counts_ready if layer == 0 else sums_ready, group_no(0, i, q))
                    dve.nop(nofuse=True)
                    added = counts_added if layer == 0 else sums_added
                    nc.vector.tensor_copy(rel_dst[:, :], where_of(g)).then_inc(added, 1)
                    dve.wait_ge(added, group_no(0, i, q))

            def where_of(g):
                return e_dst[:, bass.ds(g, 1), :].rearrange("p a q -> p (a q)")

            def norm_stats(layer, j):
                n = tile_no(layer, j)
                dve.wait_ge(residual_ready, n)
                nc.vector.bn_stats(bn[:, :], residual[:, :]).then_inc(bn_ready, 1)

            def norm_mean_var(layer, j):
                dve.wait_ge(bn_ready, tile_no(layer, j))
                dve.nop(nofuse=True)
                nc.vector.bn_aggr(mean_var, bn[:, :]).then_inc(mean_var_ready, 1)

            def norm_eps(layer, j):
                dve.wait_ge(mean_var_ready, tile_no(layer, j))
                nc.vector.tensor_scalar(var_eps, mean_var[:, 1:2], LN_EPS, None, ALU.add).then_inc(var_eps_ready, 1)

            def norm_reciprocal(layer, j):
                dve.wait_ge(std_ready, tile_no(layer, j))
                nc.vector.reciprocal(rstd, std).then_inc(rstd_ready, 1)

            def norm_result(layer, j):
                dve.wait_ge(rstd_ready, tile_no(layer, j))
                at_least(dve, x1_stored if layer == 0 else out_stored, 16 * j)
                nc.vector.tensor_scalar(result[:, :], residual[:, :], mean_var[:, 0:1], rstd,
                                        ALU.subtract, ALU.mult).then_inc(result_ready, 1)

            NORM_STEPS = {3: norm_stats, 5: norm_mean_var, 7: norm_eps, 11: norm_reciprocal, 12: norm_result}

            def layer_norm(layer, j):
                for k in sorted(NORM_STEPS):
                    NORM_STEPS[k](layer, j)

            def take_bias(j):
                cols = acc[:, bass.ds(j * P, P)]
                dve.wait_ge(bias_ready, j + 1)
                at_least(dve, proj_ready, j)
                nc.vector.tensor_tensor(agg_t[:, :], cols, node_bias, ALU.add).then_inc(agg_ready, 1)
                nc.vector.tensor_scalar(degree, node_degree, 1.0, None, ALU.max).then_inc(degree_ready, 1)
                dve.wait_ge(agg_ready, j + 1)
                dve.nop(nofuse=True)
                nc.vector.tensor_copy(cols, zeros[:, :])

            def degree_reciprocal(j):
                dve.wait_ge(root_ready, j + 1)
                nc.vector.reciprocal(degree_norm, degree_root).then_inc(norm_ready, 1)

            def add_residual(j):
                dve.wait_ge(activated_ready, j + 1)
                dve.wait_ge(node_loaded, 16 * (j + 1))
                nc.vector.tensor_tensor(residual[:, :], activated[:, :], node_x[:, :],
                                        ALU.add).then_inc(residual_ready, 1)

            def node_tile0(j):
                take_bias(j)
                degree_reciprocal(j)
                add_residual(j)
                layer_norm(0, j)

            def node_tile1(j):
                n = tile_no(1, j)
                cols = acc[:, bass.ds(j * P, P)]
                dve.wait_ge(node_t_ready, j + 1)
                at_least(dve, proj_ready, n - 1)
                nc.vector.tensor_tensor(agg_t[:, :], cols, node_bias, ALU.add)
                nc.vector.tensor_tensor(product_t[:, :], cols, node_bias,
                                        ALU.mult).then_inc(agg_ready, 1)
                dve.wait_ge(sloped_ready, j + 1)
                nc.vector.tensor_tensor(activated[:, :], node_proj, squares[:, :],
                                        ALU.max).then_inc(leaky_ready, 1)
                dve.wait_ge(length_ready, j + 1)
                nc.vector.tensor_scalar(length_floor, length, NORM_EPS, None, ALU.max).then_inc(length_floored, 1)
                dve.wait_ge(length_floored, j + 1)
                nc.vector.reciprocal(inv_length, length_floor).then_inc(inv_length_ready, 1)
                dve.wait_ge(inv_length_ready, j + 1)
                nc.vector.scalar_tensor_tensor(residual[:, :], activated[:, :], inv_length, node_x[:, :],
                                               ALU.mult, ALU.add).then_inc(residual_ready, 1)
                layer_norm(1, j)

            def finish1():
                for q in range(ITER_GROUPS):
                    add_sums(ITERS - 1, q)
                dve.wait_ge(sums_added, GROUPS)

            fast_or_general(dve, nc.vector,
                            lambda: run_fast_pairs(dve, LAGS[0], iteration0, node_tile0, finish0),
                            lambda: run_general(dve, lambda i: general_iteration(0, i), node_tile0))
            fast_or_general(dve, nc.vector,
                            lambda: run_fast(dve, LAGS[1], iteration, node_tile1, finish1),
                            lambda: run_general(dve, lambda i: general_iteration(1, i), node_tile1))

        @block.tensor
        def _(pe):
            pe.wait_ge(consts_set, 8)
            pe.wait_ge(floats_ready, 1)
            for n, (a, b) in enumerate(PREP):
                at_least(pe, prep_stored_dve if n % 2 else prep_stored_act, (n - 8) // 2 + 1)
                for q in range(GROUP_TILES):
                    ins = nc.tensor.transpose(psum[:, n % 8, q * P:(q + 1) * P],
                                              prep_in[a][b][:, q * P:(q + 1) * P], identity[:, :])
                ins.then_inc(prep_transposed, 1)
            pe.wait_ge(over_ready, 1)
            pe.wait_ge(prep_stored_act, len(PREP) // 2)
            pe.wait_ge(prep_stored_dve, len(PREP) // 2)
            nc.tensor.matmul(psum[0:1, SUM_BANK, 0:GROUP_BLOCKS * SPANS], ones[:, 0:1],
                             span_over[:, :, :].rearrange("p b s -> p (b s)"), start=True, stop=True
                             ).then_inc(over_summed, 1)
            pe.wait_ge(weights_in, 16 * 7)
            pe.wait_ge(general_set, 1)

            def group_sums(k0, hot, slots_ready):
                bank = k0 // GROUP_TILES % RING
                for k in range(GROUP_TILES):
                    slots_ready(k0 + k)
                    ins = nc.tensor.matmul(psum[:, bank, 0:WINDOW], gathered[:, k0 + k, :], hot[:, k, :],
                                           start=(k == 0), stop=(k == GROUP_TILES - 1))
                return ins

            def group_counts(q):
                for k in range(GROUP_TILES):
                    ins = nc.tensor.matmul(count_sums(q),
                                           type_onehot[:, q, k, :], dst_onehot[:, q, k, :],
                                           start=(k == 0), stop=(k == GROUP_TILES - 1))
                return ins

            def iteration(i):
                for q in range(ITER_GROUPS):
                    pe.wait_ge(onehot_ready, group_no(1, i, q))
                    at_least(pe, sums_added, group_no(0, i, q) - ITER_GROUPS)
                    group_sums(q * GROUP_TILES, onehot[:, q, :, :],
                               lambda k: pe.wait_ge(gather_done[k], 16 * (ITERS + i + 1))).then_inc(sums_ready, 1)

            def relations(i, s, r0, r1):
                for r in range(r0, r1):
                    ins = nc.tensor.matmul(psum[:, SUM_BANK, 0:ITER_WINDOW], relation_w[:, r * D:(r + 1) * D],
                                           sums[:, s, r * ITER_WINDOW:(r + 1) * ITER_WINDOW],
                                           start=(r == 0), stop=(r == R - 1))
                    if (r + 1) % (R // CLEAR_PARTS) == 0:
                        ins.then_inc(iter_products_part, 1)

            def iteration0(i, s, j, last_j):
                first = isinstance(i, int) and i == 0
                relation = 0
                for k in range(SLOTS):
                    if j is not None and k == 1:
                        bias_products(j)
                    if j is not None and k == 6:
                        loop_product(j)
                    pe.wait_ge(gather_done[k], 16 * (i + 1))
                    if k in ACT_ONEHOTS:
                        pe.wait_ge(joint_ready_act, i * len(ACT_ONEHOTS) + ACT_ONEHOTS.index(k) + 1)
                    else:
                        pe.wait_ge(joint_ready_dve, i * len(DVE_ONEHOTS) + DVE_ONEHOTS.index(k) + 1)
                    at_least(pe, tile_added, tile_count(i, k) - RING)
                    for part in range(2):
                        ins = nc.tensor.matmul(psum[:, k % RING, 0:JOINT], gathered_parts[:, k, part, :],
                                               joint_onehot[:, k % ADD_LAG, :], start=(part == 0),
                                               stop=(part == 1))
                    ins.then_inc(tile_sums_ready, 1)
                    if k % GROUP_TILES == GROUP_TILES - 1:
                        q = k // GROUP_TILES
                        pe.wait_ge(onehot_ready, group_no(0, i, q))
                        at_least(pe, counts_added, group_no(0, i, q) - 2)
                        group_counts(q).then_inc(counts_ready, 1)
                    if not first and k in RELATIONS_BEHIND:
                        if relation == 0:
                            pe.wait_ge(tile_added, i * SLOTS)
                            at_least(pe, iter_added, i - 1)
                        relations(i - 1, 1 - s, relation, relation + RELATIONS_BEHIND[k])
                        relation += RELATIONS_BEHIND[k]

            def finish0():
                pe.wait_ge(tile_added, TILES)
                pe.wait_ge(iter_added, ITERS - 1)
                relations(ITERS - 1, 1, 0, R)

            def messages(i, q):
                for k in range(GROUP_TILES):
                    n = (i * ITER_GROUPS + q) * GROUP_TILES + k
                    pe.wait_ge(parts_summed, n + 1)
                    nc.tensor.transpose(node_bias, residual[:, :], identity[:, :]
                                        ).then_inc(message_x_t, 1)
                    pe.wait_ge(message_x_t_ready, n + 1)
                    for c in range(CHUNKS):
                        at_least(pe, message_step, n * R + (c - 1) * CHUNK_RELATIONS)
                        nc.tensor.matmul(psum[:, c % 2, :], agg_t[:, :], relation_w[:, c * BANK:(c + 1) * BANK],
                                         start=True, stop=True).then_inc(products_ready, 1)
                pe.wait_ge(message_step, (i * ITER_GROUPS + q + 1) * GROUP_TILES * R)

            def general_iteration(layer, i):
                for q in range(ITER_GROUPS):
                    g = i * ITER_GROUPS + q
                    for k in range(q * GROUP_TILES, (q + 1) * GROUP_TILES):
                        pe.wait_ge(gather_done[k], 16 * (layer * ITERS + i + 1))
                    if layer == 0:
                        messages(i, q)

                    def window(w):
                        n = (layer * GROUPS + g) * WINDOWS + w
                        pe.wait_ge(gen_onehot_ready, n + 1)
                        at_least(pe, gen_added, n)
                        for k in range(GROUP_TILES):
                            ins = nc.tensor.matmul(psum[:, 0, 0:WINDOW], gathered[:, q * GROUP_TILES + k, :],
                                                   onehot[:, 0, k, :], start=(k == 0),
                                                   stop=(k == GROUP_TILES - 1))
                        if layer == 0:
                            ins = group_counts(0)
                        ins.then_inc(gen_sum_ready, 1)

                    window(0)
                    with pe.Fori(1, WINDOWS - 1) as w:
                        window(w)
                    window(WINDOWS - 1)
                    nc.tensor.matmul(psum[:, 1, 0:WINDOW], gathered[:, q * GROUP_TILES, :], onehot[:, 0, 0, :],
                                     start=True, stop=True).then_inc(counts_ready if layer == 0 else sums_ready, 1)
                    if layer == 0 and q % 2:
                        nc.tensor.matmul(psum[:, 2, 0:WINDOW], gathered[:, q * GROUP_TILES, :],
                                         onehot[:, 0, 0, :], start=True, stop=True).then_inc(tile_sums_ready, SLOTS // 2)

            def bias_products(j):
                pe.wait_ge(count_tile_ready, j + 1)
                at_least(pe, activated_ready, j)
                nc.tensor.matmul(node_bias, r_feat[:, :], count_tile[:, :], start=True, stop=True)
                nc.tensor.matmul(node_degree, count_tile[:, :], ones[0:R, 0:1],
                                 start=True, stop=True).then_inc(bias_ready, 1)

            def loop_product(j):
                pe.wait_ge(agg_ready, j + 1)
                pe.wait_ge(degree_ready, j + 1)
                nc.tensor.matmul(node_proj, agg_t[:, :], loop_plus_i[:, :],
                                 start=True, stop=True).then_inc(proj_ready, 1)

            def node_tile0(j):
                bias_products(j)
                loop_product(j)

            def node_tile1(j):
                n = tile_no(1, j)
                pe.wait_ge(node_loaded, 16 * n)
                pe.wait_ge(activated_ready, NODE_TILES)
                at_least(pe, leaky_ready, j)
                nc.tensor.transpose(node_bias, node_x[:, :], identity[:, :]).then_inc(node_t_ready, 1)
                pe.wait_ge(agg_ready, n)
                nc.tensor.matmul(node_proj, agg_t[:, :], w1_sb[:, :], start=True, stop=False)
                nc.tensor.matmul(node_proj, product_t[:, :], w2_sb[:, :], start=False, stop=False)
                nc.tensor.matmul(node_proj, ones[0:1, :], b12_sb[:, :],
                                 start=False, stop=True).then_inc(proj_ready, 1)

            fast_or_general(pe, nc.tensor,
                            lambda: run_fast_pairs(pe, LAGS[0], iteration0, node_tile0, finish0),
                            lambda: run_general(pe, lambda i: general_iteration(0, i), node_tile0))
            fast_or_general(pe, nc.tensor,
                            lambda: run_fast(pe, LAGS[1], iteration, node_tile1, lambda: None, tile_first=True),
                            lambda: run_general(pe, lambda i: general_iteration(1, i), node_tile1))


_INS = ["x", "src", "dst", "edge_type_40", "edge_weight", "L0_gnn_rFeatures", "L0_gnn_relation_weights",
        "L0_gnn_loop_weight", "L1_gnn_W1", "L1_gnn_W2", "L1_gnn_b1", "L1_gnn_b2"]


def kernel(**inputs):
    import numpy as _np
    import concourse.bacc as _bacc
    from concourse import mybir as _mybir
    from concourse.bass_utils import run_bass_kernel_spmd as _run

    nc = _bacc.Bacc("TRN2", target_bir_lowering=False, num_devices=1)
    arrays, args = {}, []
    for name in _INS:
        a = _np.ascontiguousarray(inputs[name])
        arrays[f"in_{name}_dram"] = a
        args.append(nc.dram_tensor(f"in_{name}_dram", a.shape, _mybir.dt.from_np(a.dtype), kind="ExternalInput").ap())
    shape = inputs["x"].shape
    args.append(nc.dram_tensor("out_dram", shape, _mybir.dt.float32, kind="ExternalOutput").ap())
    build(nc, *args)
    r = _run(nc, [arrays], core_ids=[0])
    return r.results[0]["out_dram"]
```

```python
from contextlib import ExitStack

import concourse.bass as bass
from concourse import mybir

ALU = mybir.AluOpType
ACT = mybir.ActivationFunctionType
AX_X = mybir.AxisListType.X
F32 = mybir.dt.float32
F32R = mybir.dt.float32r
BF16 = mybir.dt.bfloat16
I32 = mybir.dt.int32

P = 128
TILE_EDGES = P
GROUP_TILES = 4
GROUP_EDGES = GROUP_TILES * TILE_EDGES
ITER_GROUPS = 4
SLOTS = ITER_GROUPS * GROUP_TILES
WINDOW = 64
TILE_WINDOW = 12
ITER_WINDOW = 136
LAGS = (6, 5)
ADD_LAG = 8
ACT_ONEHOTS = (1, 3, 5, 7, 9, 11, 13, 15)
RELATIONS_BEHIND = {**{k: 4 for k in range(3, 10)}, **{k: 3 for k in range(10, 14)}}
ROW_PARTS = (4, 2)
CLEAR_PARTS = 4
CLEARS = {1: 0, 3: 1, 5: 2, 7: 3}
SPLIT_TILES = 7
NO_TYPE = 1 << 10
NO_NODE = 1 << 20
LN_EPS = 1e-5
NORM_EPS = 1e-12
SLOPE = 0.2
BANK = 512


def at_least(eng, sem, count):
    if not isinstance(count, int) or count > 0:
        eng.wait_ge(sem, count)


def build(nc, x, src, dst, edge_type, edge_weight, r_features, r_weights, loop_weight,
          w1, w2, b1, b2, out):
    N, D = x.shape
    E = src.shape[0]
    R = r_weights.shape[0]
    assert D == P
    NODE_TILES = -(-N // P)
    LAST_ROWS = N - (NODE_TILES - 1) * P
    NP = NODE_TILES * P
    GROUPS = -(-E // (ITER_GROUPS * GROUP_EDGES)) * ITER_GROUPS
    ITERS = GROUPS // ITER_GROUPS
    GROUP_BLOCKS = -(-GROUPS // P)
    ACC_COLS = NP + ITER_WINDOW
    TILES = ITERS * SLOTS
    JOINT = R * TILE_WINDOW
    BLOCKS = R + 1
    S_COLS = BLOCKS * ITER_WINDOW
    DVE_ONEHOTS = tuple(k for k in range(SLOTS) if k not in ACT_ONEHOTS)
    WINDOWS = -(-N // WINDOW)
    CHUNKS = R * D // BANK
    CHUNK_RELATIONS = BANK // D
    SPLIT_STEPS = NODE_TILES // SPLIT_TILES
    assert 2 * SPLIT_TILES <= SLOTS
    assert BLOCKS * TILE_WINDOW <= BANK and sum(RELATIONS_BEHIND.values()) == R and R % CLEAR_PARTS == 0
    assert N > (NODE_TILES - 1) * P and N % SPLIT_TILES and ITERS % 2 == 0 and LAGS[0] % 2 == 0
    assert GROUPS == -(-E // GROUP_EDGES) and GROUP_BLOCKS == 2 and NODE_TILES % SPLIT_TILES == 0

    x_split = nc.dram_tensor("x_split", [N, 2 * D], F32, kind="Internal").ap()
    x1_rows = nc.dram_tensor("layer0_result", [N, D], F32, kind="Internal").ap()

    SPANS = 5

    with ExitStack() as ctx:
        def sb(name, shape, dt=F32):
            return ctx.enter_context(nc.sbuf_tensor(name, shape, dt))

        def sem(name):
            return ctx.enter_context(nc.semaphore(name))

        identity = sb("identity", [P, P])
        ones = sb("ones", [P, P])
        zeros_wide = sb("zeros_wide", [P, ITER_WINDOW])
        window_iota = sb("window_iota", [P, WINDOW])
        type_iota = sb("type_iota", [P, R])
        group_floor = sb("group_floor", [P, GROUP_BLOCKS])
        joint_iota = sb("joint_iota", [P, JOINT])
        relation_w = sb("relation_w", [P, R * D])
        r_feat = sb("r_feat", [R, D])
        loop_w = sb("loop_w", [P, D])
        loop_plus_i = sb("loop_plus_i", [P, D + 1])
        r_feat_t = sb("r_feat_t", [P, R])
        r_loop = sb("r_loop", [R, D + 1])
        w1_sb = sb("w1_sb", [P, D])
        w2_sb = sb("w2_sb", [P, D])
        b1_sb = sb("b1_sb", [1, D])
        b2_sb = sb("b2_sb", [1, D])
        b12_sb = sb("b12_sb", [1, D])
        E_SHAPE = [P, GROUPS, GROUP_TILES]
        e_joint = sb("e_joint", E_SHAPE)
        e_src = sb("e_src", E_SHAPE)
        e_type = sb("e_type", E_SHAPE)
        e_local = sb("e_local", E_SHAPE)
        e_dst = sb("e_dst", E_SHAPE)
        e_weight = sb("e_weight", E_SHAPE)
        group_base = sb("group_base", [1, GROUPS], I32)
        tile_base = sb("tile_base", [1, ITERS, SLOTS], I32)
        tile_base_f = sb("tile_base_f", [1, ITERS, SLOTS])
        tile_offset_f = sb("tile_offset_f", [1, ITERS, SLOTS])
        tile_offset = sb("tile_offset", [1, ITERS, SLOTS], I32)
        offset_span = sb("offset_span", [1, 2])
        offset_over = sb("offset_over", [1, 2])
        sums = sb("sums", [P, 2, S_COLS])
        scratch = sums[:, :, :].rearrange("p s c -> p (s c)")

        def raw(n):
            return scratch[:, n * GROUP_EDGES:(n + 1) * GROUP_EDGES]

        raw_src = [raw(0).bitcast(I32), raw(1).bitcast(I32)]
        raw_dst = [raw(2).bitcast(I32), raw(3).bitcast(I32)]
        raw_type = [raw(4).bitcast(I32), raw(5).bitcast(I32)]
        raw_weight = [raw(6), raw(7)]
        f_src = [raw(8), raw(9)]
        f_dst = [raw(10), raw(11)]
        f_type = [raw(12), raw(13)]
        f_local = [raw(14), raw(15)]
        f_joint = [raw(16), raw(17)]
        f_inside = [raw(18), raw(19)]
        f_tile_local = [raw(2), raw(3)]
        span = sb("span", [P, GROUP_BLOCKS, SPANS])
        span_over = sb("span_over", [P, GROUP_BLOCKS, SPANS])
        over_sum = sb("over_sum", [1, 3])
        general = sb("general", [1, 1], I32)

        gathered_parts = sb("gathered_parts", [P, SLOTS, 2, D], F32R)
        gathered = sb("gathered", [P, SLOTS, D])
        x_in = [gathered[:, b * SPLIT_TILES:(b + 1) * SPLIT_TILES, :] for b in range(2)]
        x_parts = [gathered_parts[:, b * SPLIT_TILES:(b + 1) * SPLIT_TILES, :, :] for b in range(2)]
        joint_onehot = sb("joint_onehot", [P, ADD_LAG, JOINT], F32R)
        distance = sb("distance", [P, JOINT])
        gather_rows = sb("gather_rows", [P, SLOTS], I32)
        ONEHOTS = SLOTS * WINDOW
        onehot = scratch[:, 0:ONEHOTS].rearrange("p (g q w) -> p g q w", g=ITER_GROUPS, q=GROUP_TILES)
        type_onehot = sb("type_onehot", [P, SLOTS, R], BF16)
        tile_local = sb("tile_local", [P, SLOTS])
        tile_dst_onehot = sb("tile_dst_onehot", [P, SLOTS, TILE_WINDOW], BF16)
        dst_onehot = scratch[:, ONEHOTS:ONEHOTS + GROUP_TILES * WINDOW // 2].bitcast(BF16).rearrange(
            "p (q w) -> p q w", q=GROUP_TILES)
        rel_dst = sb("rel_dst", [P, GROUP_TILES])
        acc = sb("acc", [P, ACC_COLS])
        counts_rows = sb("counts", [P, ACC_COLS])
        counts = counts_rows[0:R, :]

        node_x = sb("node_x", [P, D])
        count_tile = sb("count_tile", [R, P])
        agg_t = sb("agg_t", [P, P])
        product_t = sb("product_t", [P, P])
        type_mask = sb("type_mask", [P, R])
        small = sb("small", [P, 16])
        degree, degree_root, degree_norm = small[:, 0:1], small[:, 1:2], small[:, 2:3]
        var_eps, std, rstd = small[:, 3:4], small[:, 4:5], small[:, 5:6]
        square_sum, length, length_floor, inv_length = (
            small[:, 6:7], small[:, 7:8], small[:, 8:9], small[:, 9:10])
        mean_var = small[:, 10:12]
        bn = sb("bn", [P, 6])
        activated = sb("activated", [P, D])
        squares = sb("squares", [P, D])
        residual = sb("residual", [P, D])
        result = sb("result", [P, D])

        psum = ctx.enter_context(nc.psum_tensor("psum", [P, 8, BANK], F32))
        RING = (0, 1, 2, 3, 5, 7)

        def tile_bank(k):
            return RING[(k + SLOTS // 2) % SLOTS % len(RING)]

        def tiles_back(k):
            return next(n for n in range(1, SLOTS) if tile_bank(k - n) == tile_bank(k))

        SUM_BANK, NODE_BANK, COUNT_BANK = 4, 6, 5
        node_proj = psum[:, NODE_BANK, 0:D]
        node_degree = psum[:, NODE_BANK, D:D + 1]
        node_t = psum[:, NODE_BANK, 2 * P:3 * P]

        count_sums = psum[0:R, COUNT_BANK, 0:WINDOW]

        weights_in = sem("weights_in")
        relation_w_in = sem("relation_w_in")
        loop_plus_ready = sem("loop_plus_ready")
        r_feat_transposed = sem("r_feat_transposed")
        r_loop_product = sem("r_loop_product")
        edges_in = sem("edges_in")
        base_in = sem("base_in")
        pad_set = sem("pad_set")
        consts_set = sem("consts_set")
        dve_prep = sem("dve_prep")
        floats_ready = sem("floats_ready")
        prep_transposed = sem("prep_transposed")
        prep_stored_act = sem("prep_stored_act")
        prep_stored_dve = sem("prep_stored_dve")
        over_ready = sem("over_ready")
        over_summed = sem("over_summed")
        general_set = sem("general_set")
        x_loaded = [sem(f"x_loaded{b}") for b in range(2)]
        x_high_ready = sem("x_high_ready")
        x_low_ready = sem("x_low_ready")
        parts_stored = [sem(f"parts_stored{b}") for b in range(2)]
        joint_ready_dve = sem("joint_ready_dve")
        joint_ready_act = sem("joint_ready_act")
        distance_ready = sem("distance_ready")
        tile_sums_ready = sem("tile_sums_ready")
        tile_added = sem("tile_added")
        sums_cleared = sem("sums_cleared")
        iter_products_part = sem("iter_products_part")
        mask_ready = sem("mask_ready")
        message_step = sem("message_step")
        iter_added = sem("iter_added")
        counts_ready = sem("counts_ready")
        counts_added = sem("counts_added")
        offsets_set = sem("offsets_set")
        parts_summed = sem("parts_summed")
        message_x_t = sem("message_x_t")
        message_x_t_ready = sem("message_x_t_ready")
        products_ready = sem("products_ready")
        rows_ready = sem("rows_ready")
        gather_done = [sem(f"gather_done{k}") for k in range(SLOTS)]
        onehot_eq = sem("onehot_eq")
        tile_local_ready = sem("tile_local_ready")
        count_onehots_ready = sem("count_onehots_ready")
        iter_counts_added = sem("iter_counts_added")
        onehot_ready = sem("onehot_ready")
        sums_ready = sem("sums_ready")
        sums_added = sem("sums_added")
        gen_rel = sem("gen_rel")
        gen_eq = sem("gen_eq")
        gen_onehot_ready = sem("gen_onehot_ready")
        gen_sum_ready = sem("gen_sum_ready")
        gen_added = sem("gen_added")
        acc_cleared = sem("acc_cleared")
        zeros_wide_set = sem("zeros_wide_set")
        count_tile_ready = sem("count_tile_ready")
        agg_ready = sem("agg_ready")
        degree_ready = sem("degree_ready")
        root_ready = sem("root_ready")
        norm_ready = sem("norm_ready")
        proj_ready = sem("proj_ready")
        activated_ready = sem("activated_ready")
        sloped_ready = sem("sloped_ready")
        leaky_ready = sem("leaky_ready")
        squares_ready = sem("squares_ready")
        length_ready = sem("length_ready")
        length_floored = sem("length_floored")
        inv_length_ready = sem("inv_length_ready")
        node_loaded = sem("node_loaded")
        node_t_ready = sem("node_t_ready")
        residual_ready = sem("residual_ready")
        bn_ready = sem("bn_ready")
        mean_var_ready = sem("mean_var_ready")
        var_eps_ready = sem("var_eps_ready")
        std_ready = sem("std_ready")
        rstd_ready = sem("rstd_ready")
        result_ready = sem("result_ready")
        x1_stored = sem("x1_stored")
        out_stored = sem("out_stored")

        def group_no(i, q):
            return i * ITER_GROUPS + q + 1

        def tile_no(layer, j):
            return layer * NODE_TILES + j + 1

        def row_parts(layer, i, h):
            return layer * ROW_PARTS[0] * ITERS + ROW_PARTS[layer] * i + h + 1

        def part_slots(layer, h):
            size = SLOTS // ROW_PARTS[layer]
            return range(h * size, (h + 1) * size)

        def split_dmas(step):
            return step // 2 + 1 + (step == SPLIT_STEPS - 1)

        PREP = [(a, b) for a in range(6) for b in range(GROUP_BLOCKS)]
        prep_in = [f_joint, f_src, f_type, f_local, f_dst, raw_weight]
        prep_out = [e_joint, e_src, e_type, e_local, e_dst, e_weight]

        def fast_or_general(eng, engine, fast, slow):
            eng.wait_ge(general_set, 1)
            flag = engine.value_load(general[0:1, 0:1], min_val=0, max_val=1)
            with eng.If(flag < 1):
                fast()
            with eng.Else():
                slow()

        def tile_count(i, k):
            return i * SLOTS + k + 1

        def run_fast(eng, lag, iteration, node_tile, finish, tile_first=False):
            def both(i):
                if tile_first:
                    node_tile(i - lag)
                iteration(i)
                if not tile_first:
                    node_tile(i - lag)

            iteration(0)
            with eng.Fori(1, lag) as i:
                iteration(i)
            both(lag)
            with eng.Fori(lag + 1, ITERS) as i:
                both(i)
            finish()
            for j in range(ITERS - lag, NODE_TILES):
                node_tile(j)

        def run_fast_pairs(eng, lag, iteration, node_tile, finish):
            def pair(p, with_tiles):
                for s in range(2):
                    i = 2 * p + s
                    has_last = with_tiles and not (isinstance(i, int) and i == lag)
                    iteration(i, s, i - lag if with_tiles else None, i - lag - 1 if has_last else None)

            pair(0, False)
            with eng.Fori(1, lag // 2) as p:
                pair(p, False)
            pair(lag // 2, True)
            with eng.Fori(lag // 2 + 1, ITERS // 2) as p:
                pair(p, True)
            finish(ITERS - lag)
            for j in range(ITERS - lag + 1, NODE_TILES):
                node_tile(j)

        def run_general(eng, iteration, node_tile):
            iteration(0)
            with eng.Fori(1, ITERS) as i:
                iteration(i)
            node_tile(0)
            with eng.Fori(1, NODE_TILES) as j:
                node_tile(j)

        block = ctx.enter_context(nc.Block())

        @block.sync
        def _(sp):
            def load_edges():
                FULL = E // GROUP_EDGES
                for b in range(GROUP_BLOCKS):
                    g0, g1 = b * P, min((b + 1) * P, FULL)
                    for dram, tiles in ((dst, raw_dst), (src, raw_src), (edge_type, raw_type),
                                        (edge_weight, raw_weight)):
                        sp.dma_start(tiles[b][0:g1 - g0, :],
                                     dram[g0 * GROUP_EDGES:g1 * GROUP_EDGES].rearrange(
                                         "(g e) -> g e", e=GROUP_EDGES)).then_inc(edges_in, 16)
                rest = E - FULL * GROUP_EDGES
                for dram, tiles in ((dst, raw_dst), (src, raw_src), (edge_type, raw_type),
                                    (edge_weight, raw_weight)):
                    sp.dma_start(tiles[-1][FULL % P:FULL % P + 1, 0:rest],
                                 dram[FULL * GROUP_EDGES:E].rearrange("(g e) -> g e", g=1)).then_inc(edges_in, 16)

            def load_weights():
                sp.dma_start(r_feat[:, :], r_features).then_inc(weights_in, 16)
                sp.dma_start(loop_w[:, :], loop_weight).then_inc(weights_in, 16)
                sp.dma_start(w1_sb[:, :], w1).then_inc(weights_in, 16)
                sp.dma_start(w2_sb[:, :], w2).then_inc(weights_in, 16)
                sp.dma_start(b1_sb[:, :], b1).then_inc(weights_in, 16)
                sp.dma_start(b2_sb[:, :], b2).then_inc(weights_in, 16)

            def split_rows(step):
                r0 = step * SPLIT_TILES * P
                full = min(P, (N - r0) // SPLIT_TILES)
                rest = 0 if full == P else N - r0 - full * SPLIT_TILES
                yield slice(r0, r0 + full * SPLIT_TILES), slice(0, full), slice(0, SPLIT_TILES)
                if rest:
                    yield slice(N - rest, N), slice(full, full + 1), slice(0, rest)

            def load_x(step):
                if step >= 2:
                    sp.wait_ge(x_high_ready, step - 1)
                    sp.wait_ge(x_low_ready, step - 1)
                for rows, parts, places in split_rows(step):
                    sp.dma_start(x_in[step % 2][parts, places, :],
                                 x[rows, :].rearrange("(p t) d -> p t d", p=parts.stop - parts.start)
                                 ).then_inc(x_loaded[step % 2], 16)

            def store_parts(step):
                sp.wait_ge(x_high_ready, step + 1)
                sp.wait_ge(x_low_ready, step + 1)
                for rows, parts, places in split_rows(step):
                    sp.dma_start(x_split[rows, :].rearrange("(p t) d -> p t d", p=parts.stop - parts.start),
                                 x_parts[step % 2][parts, places, :, :].rearrange("p t a d -> p t (a d)").bitcast(F32)
                                 ).then_inc(parts_stored[step % 2], 16)

            load_x(0)
            load_x(1)
            sp.wait_ge(pad_set, 5)
            load_edges()
            for step in range(SPLIT_STEPS):
                store_parts(step)
                if step + 2 < SPLIT_STEPS:
                    load_x(step + 2)
                if step == SPLIT_STEPS - 4:
                    load_weights()
            sp.dma_start(relation_w[:, :].rearrange("p (r f) -> p r f", r=R),
                         r_weights.rearrange("r d f -> d r f")).then_inc(relation_w_in, 16)

            def node_rows(j):
                last = isinstance(j, int) and j == NODE_TILES - 1
                return (slice(j * P, N), LAST_ROWS) if last else (bass.ds(j * P, P), P)

            def load_node(layer, j):
                rows, n = node_rows(j)
                at_least(sp, residual_ready, tile_no(layer, j) - 1)
                sp.dma_start(node_x[0:n, :], (x, x1_rows)[layer][rows, :]).then_inc(node_loaded, 16)

            def store_node(layer, j):
                rows, n = node_rows(j)
                sp.wait_ge(result_ready, tile_no(layer, j))
                sp.dma_start((x1_rows, out)[layer][rows, :], result[0:n, :]).then_inc(
                    (x1_stored, out_stored)[layer], 16)

            for layer in range(2):
                if layer == 1:
                    sp.wait_ge(x1_stored, 16 * NODE_TILES)
                load_node(layer, 0)
                with sp.Fori(0, NODE_TILES - 2) as j:
                    load_node(layer, j + 1)
                    store_node(layer, j)
                load_node(layer, NODE_TILES - 1)
                store_node(layer, NODE_TILES - 2)
                store_node(layer, NODE_TILES - 1)
            sp.wait_ge(out_stored, 16 * NODE_TILES)

        @block.gpsimd
        def _(pool):
            nc.gpsimd.memset(raw_dst[1], NO_NODE).then_inc(pad_set, 1)
            nc.gpsimd.memset(raw_src[1], 0).then_inc(pad_set, 1)
            nc.gpsimd.memset(raw_type[1], NO_TYPE).then_inc(pad_set, 1)
            nc.gpsimd.memset(raw_weight[1], 0.0).then_inc(pad_set, 1)
            nc.gpsimd.memset(tile_base[:, :, :], 0).then_inc(pad_set, 1)
            nc.gpsimd.memset(ones[:, :], 1.0).then_inc(consts_set, 1)
            nc.gpsimd.memset(identity[:, :], 0.0).then_inc(consts_set, 1)
            nc.gpsimd.iota(window_iota[:, :], pattern=[[1, WINDOW]], base=0, channel_multiplier=0,
                           allow_small_or_imprecise_dtypes=True).then_inc(consts_set, 1)
            nc.gpsimd.iota(type_iota[:, :], pattern=[[1, R]], base=0, channel_multiplier=0,
                           allow_small_or_imprecise_dtypes=True).then_inc(consts_set, 1)
            nc.gpsimd.iota(joint_iota[:, :], pattern=[[1, JOINT]], base=0, channel_multiplier=0,
                           allow_small_or_imprecise_dtypes=True).then_inc(consts_set, 1)
            nc.gpsimd.iota(group_floor[:, :], pattern=[[P // ITER_GROUPS * P, GROUP_BLOCKS]],
                           base=-P * (LAGS[1] - 1), channel_multiplier=P // ITER_GROUPS,
                           allow_small_or_imprecise_dtypes=True).then_inc(consts_set, 1)
            pool.wait_ge(consts_set, 6)
            nc.gpsimd.affine_select(out=identity[:, :], in_=identity[:, :], compare_op=ALU.not_equal, fill=1.0,
                                    base=0, pattern=[[-1, P]], channel_multiplier=1).then_inc(consts_set, 1)

            nc.gpsimd.memset(acc[:, :], 0.0).then_inc(acc_cleared, 1)
            nc.gpsimd.memset(counts_rows[:, :], 0.0).then_inc(acc_cleared, 1)

            def iteration(layer, i):
                rows, slots = (x_split, gathered_parts[:, :, :, :].rearrange("p s a d -> p s (a d)").bitcast(F32)
                               ) if layer == 0 else (x1_rows, gathered[:, :, :])
                for h in range(ROW_PARTS[layer]):
                    pool.wait_ge(rows_ready, row_parts(layer, i, h))
                    pool.nop(nofuse=True)
                    for k in part_slots(layer, h):
                        nc.gpsimd.indirect_dma_start(
                            slots[:, k, :], None, rows,
                            bass.IndirectOffsetOnAxis(ap=gather_rows[:, k:k + 1], axis=0),
                        ).then_inc(gather_done[k], 16)

            for layer in range(2):
                if layer == 0:
                    for step in (SPLIT_STEPS - 2, SPLIT_STEPS - 1):
                        pool.wait_ge(parts_stored[step % 2], 16 * split_dmas(step))
                else:
                    pool.wait_ge(agg_ready, NODE_TILES - 3)
                    nc.gpsimd.memset(acc[:, 0:(NODE_TILES - 3) * P], 0.0).then_inc(acc_cleared, 1)
                    pool.wait_ge(agg_ready, NODE_TILES)
                    nc.gpsimd.memset(acc[:, (NODE_TILES - 3) * P:ACC_COLS], 0.0).then_inc(acc_cleared, 1)
                    pool.wait_ge(x1_stored, 16 * NODE_TILES)
                with pool.Fori(0, ITERS) as i:
                    iteration(layer, i)

        @block.scalar
        def _(act):
            FIRSTS = -(-E // TILE_EDGES)
            act.wait_ge(pad_set, 5)
            act.dma_start(tile_base[:, :, :].rearrange("a i k -> a (i k)")[:, 0:FIRSTS],
                          dst.rearrange("(a n) -> a n", a=1)[:, 0:E:TILE_EDGES],
                          allow_slow_non_contiguous=True).then_inc(base_in, 16)

            def split_high(step):
                at_least(act, parts_stored[step % 2], 16 * (step // 2))
                act.wait_ge(x_loaded[step % 2], 16 * split_dmas(step))
                nc.scalar.copy(x_parts[step % 2][:, :, 0, :], x_in[step % 2][:, :, :]).then_inc(x_high_ready, 1)

            def store_prep(n):
                a, b = PREP[n]
                act.wait_ge(prep_transposed, n + 1)
                g0, g1 = b * P, min((b + 1) * P, GROUPS)
                nc.scalar.copy(prep_out[a][:, g0:g1, :],
                               psum[:, n % 8, :].rearrange("p (q g) -> p g q", q=GROUP_TILES)[:, 0:g1 - g0, :]
                               ).then_inc(prep_stored_act, 1)

            prep_behind = {SPLIT_STEPS - 4: (0, 2, 4), SPLIT_STEPS - 3: (6, 8), SPLIT_STEPS - 1: (10,)}
            for step in range(SPLIT_STEPS):
                split_high(step)
                for n in prep_behind.get(step, ()):
                    store_prep(n)

            act.wait_ge(prep_stored_dve, len(PREP) // 2)
            act.wait_ge(zeros_wide_set, 1)

            def write_rows(layer, i, h):
                slots = part_slots(layer, h)
                groups = len(slots) // GROUP_TILES
                if layer == 0:
                    at_least(act, tile_sums_ready, tile_count(i, slots[-1]) - SLOTS)
                else:
                    at_least(act, tile_sums_ready, TILES)
                    at_least(act, sums_ready, group_no(i, groups * (h + 1) - 1) - ITER_GROUPS)
                nc.scalar.copy(gather_rows[:, slots[0]:slots[-1] + 1].rearrange("p (g q) -> p g q", q=GROUP_TILES),
                               e_src[:, bass.ds(i * ITER_GROUPS + groups * h, groups), :]).then_inc(rows_ready, 1)

            def clear_sums(i, s, part):
                at_least(act, iter_products_part, CLEAR_PARTS * (i - 2) + part + 1)
                first, end = part * R // CLEAR_PARTS, (part + 1) * R // CLEAR_PARTS
                if part == CLEAR_PARTS - 1:
                    at_least(act, iter_counts_added, i - 1)
                    end = BLOCKS
                cols = sums[:, s, first * ITER_WINDOW:end * ITER_WINDOW]
                nc.scalar.mul(cols.rearrange("p (a c) -> p a c", c=ITER_WINDOW),
                              zeros_wide[:, None, :].to_broadcast([P, end - first, ITER_WINDOW]),
                              1.0).then_inc(sums_cleared, 1)

            def iteration0(i, s, j, last_j):
                for k in range(SLOTS):
                    if k == 0:
                        write_rows(0, i, 0)
                        write_rows(0, i, 1)
                        if j is not None:
                            copy_counts(iter_counts_added, i - 1, j)
                    if k == 4:
                        write_rows(0, i, 2)
                    if k in ACT_ONEHOTS:
                        n = i * len(ACT_ONEHOTS) + ACT_ONEHOTS.index(k) + 1
                        at_least(act, joint_ready_act, n - 1)
                        key = e_joint[:, :, :].rearrange("p g q -> p (g q)")[:, bass.ds(i * SLOTS + k, 1)]
                        nc.scalar.activation(distance[:, :], joint_iota[:, :], ACT.Abs, bias=key,
                                             scale=-1.0).then_inc(distance_ready, 1)
                        if k in CLEARS:
                            clear_sums(i, s, CLEARS[k])
                        if k == 9:
                            write_rows(0, i, 3)
                        if last_j is not None and k == 11:
                            norm_sqrt(0, last_j)
                        if j is not None and k == 13:
                            degree_sqrt(j)
                        if j is not None and k == 15:
                            project_relu(j)
                        act.wait_ge(distance_ready, n)
                        at_least(act, tile_sums_ready, tile_count(i, k) - ADD_LAG)
                        nc.scalar.activation(joint_onehot[:, k % ADD_LAG, :], distance[:, :], ACT.Relu,
                                             bias=1.0, scale=-1.0).then_inc(joint_ready_act, 1)

            def iteration(layer, i):
                for h in range(ROW_PARTS[layer]):
                    write_rows(layer, i, h)

            def copy_counts(added, done, j):
                act.wait_ge(added, done)
                at_least(act, proj_ready, j)
                nc.scalar.copy(count_tile[:, :], counts[:, bass.ds(j * P, P)]).then_inc(count_tile_ready, 1)

            def degree_sqrt(j):
                act.wait_ge(degree_ready, j + 1)
                nc.scalar.activation(degree_root, degree, ACT.Sqrt).then_inc(root_ready, 1)

            def project_relu(j):
                act.wait_ge(norm_ready, j + 1)
                act.wait_ge(proj_ready, j + 1)
                nc.scalar.activation(activated[:, :], node_proj, ACT.Relu,
                                     scale=degree_norm).then_inc(activated_ready, 1)

            def norm_sqrt(layer, j):
                act.wait_ge(var_eps_ready, tile_no(layer, j))
                nc.scalar.activation(std, var_eps, ACT.Sqrt).then_inc(std_ready, 1)

            def node_tile0(added, done, j):
                copy_counts(added, done, j)
                degree_sqrt(j)
                project_relu(j)
                norm_sqrt(0, j)

            def finish0(j):
                norm_sqrt(0, j - 1)
                node_tile0(iter_counts_added, ITERS - 1, j)

            def node_tile1(j):
                act.wait_ge(proj_ready, tile_no(1, j))
                at_least(act, leaky_ready, j)
                nc.scalar.mul(squares[:, :], node_proj, SLOPE).then_inc(sloped_ready, 1)
                act.wait_ge(leaky_ready, j + 1)
                nc.scalar.activation(squares[:, :], activated[:, :], ACT.Square,
                                     accum_out=square_sum).then_inc(squares_ready, 1)
                act.wait_ge(squares_ready, j + 1)
                nc.scalar.activation(length, square_sum, ACT.Sqrt).then_inc(length_ready, 1)
                norm_sqrt(1, j)

            fast_or_general(act, nc.scalar,
                            lambda: run_fast_pairs(act, LAGS[0], iteration0,
                                                   lambda j: node_tile0(iter_counts_added, ITERS, j),
                                                   finish0),
                            lambda: run_general(act, lambda i: iteration(0, i),
                                                lambda j: node_tile0(counts_added, GROUPS, j)))
            fast_or_general(act, nc.scalar,
                            lambda: run_fast(act, LAGS[1], lambda i: iteration(1, i), node_tile1, lambda: None),
                            lambda: run_general(act, lambda i: iteration(1, i), node_tile1))

        @block.vector
        def _(dve):
            steps = [0]

            def step(ins):
                steps[0] += 1
                ins.then_inc(dve_prep, 1)
                dve.wait_ge(dve_prep, steps[0])

            def split_low(step):
                dve.wait_ge(x_high_ready, step + 1)
                nc.vector.tensor_tensor(x_parts[step % 2][:, :, 1, :], x_in[step % 2][:, :, :],
                                        x_parts[step % 2][:, :, 0, :].bitcast(F32),
                                        ALU.subtract).then_inc(x_low_ready, 1)

            def store_prep(n):
                a, b = PREP[n]
                dve.wait_ge(prep_transposed, n + 1)
                g0, g1 = b * P, min((b + 1) * P, GROUPS)
                nc.vector.tensor_copy(prep_out[a][:, g0:g1, :],
                                      psum[:, n % 8, :].rearrange("p (q g) -> p g q", q=GROUP_TILES)[:, 0:g1 - g0, :]
                                      ).then_inc(prep_stored_dve, 1)

            def edge_floats():
                dve.wait_ge(edges_in, 16 * 4 * (GROUP_BLOCKS + 1))
                for b in range(GROUP_BLOCKS):
                    nc.vector.tensor_copy(f_dst[b], raw_dst[b])
                    nc.vector.tensor_copy(f_src[b], raw_src[b])
                    ins = nc.vector.tensor_copy(f_type[b], raw_type[b])
                step(ins)

            def local_destinations():
                for b in range(GROUP_BLOCKS):
                    nc.vector.tensor_scalar(f_local[b], f_dst[b], f_dst[b][:, 0:1], None, ALU.subtract)
                    for q in range(GROUP_TILES):
                        tile = slice(q * P, (q + 1) * P)
                        ins = nc.vector.tensor_scalar(f_tile_local[b][:, tile], f_dst[b][:, tile],
                                                      f_dst[b][:, q * P:q * P + 1], None, ALU.subtract)
                step(ins)
                for b in range(GROUP_BLOCKS):
                    ins = nc.vector.scalar_tensor_tensor(f_joint[b], f_type[b], float(TILE_WINDOW), f_tile_local[b],
                                                         ALU.mult, ALU.add)
                ins.then_inc(floats_ready, 1)
                dve.wait_ge(floats_ready, 1)

            def least_destinations():
                dve.wait_ge(consts_set, 7)
                for b in range(GROUP_BLOCKS):
                    nc.vector.scalar_tensor_tensor(f_inside[b], f_local[b], float(NO_NODE // 2), f_local[b],
                                                   ALU.is_lt, ALU.mult)
                    nc.vector.tensor_reduce(span[:, b, 0:1], f_local[b], AX_X, ALU.min)
                    nc.vector.tensor_reduce(span[:, b, 3:4], f_tile_local[b], AX_X, ALU.min)
                    ins = nc.vector.tensor_tensor(span[:, b, 2:3], group_floor[:, b:b + 1], f_dst[b][:, 0:1],
                                                  ALU.subtract)
                step(ins)

            def greatest_destinations():
                for b in range(GROUP_BLOCKS):
                    ins = nc.vector.tensor_reduce(span[:, b, 1:2], f_inside[b], AX_X, ALU.max)
                step(ins)
                for b in range(GROUP_BLOCKS):
                    ins = nc.vector.scalar_tensor_tensor(f_inside[b], f_tile_local[b], float(NO_NODE // 2),
                                                         f_tile_local[b], ALU.is_lt, ALU.mult)
                step(ins)
                for b in range(GROUP_BLOCKS):
                    ins = nc.vector.tensor_reduce(span[:, b, 4:5], f_inside[b], AX_X, ALU.max)
                step(ins)

            def test_spans():
                for b in range(GROUP_BLOCKS):
                    for n, (bound, op) in enumerate(((0.0, ALU.is_lt), (float(WINDOW), ALU.is_ge), (0.0, ALU.is_gt),
                                                     (0.0, ALU.is_lt), (float(TILE_WINDOW), ALU.is_ge))):
                        ins = nc.vector.tensor_scalar(span_over[:, b, n:n + 1], span[:, b, n:n + 1], bound, None, op)
                ins.then_inc(over_ready, 1)

            def relation_biases():
                dve.wait_ge(weights_in, 16 * 6)
                nc.vector.memset(loop_plus_i[:, D:D + 1], 0.0)
                nc.vector.memset(r_loop[:, D:D + 1], 1.0)
                nc.vector.tensor_tensor(loop_plus_i[:, 0:D], loop_w[:, :], identity[:, :], ALU.add)
                dve.wait_ge(r_feat_transposed, 1)
                nc.vector.tensor_copy(r_feat_t[:, :], psum[:, NODE_BANK, 0:R]).then_inc(loop_plus_ready, 1)

            def tile_offsets():
                dve.wait_ge(base_in, 16)
                step(nc.vector.tensor_copy(tile_base_f[:, :, :], tile_base[:, :, :]))
                step(nc.vector.tensor_tensor(tile_offset_f[:, :, :], tile_base_f[:, :, :],
                                             tile_base_f[:, :, 0:1].to_broadcast([1, ITERS, SLOTS]), ALU.subtract))
                nc.vector.tensor_scalar(group_base[:, :], tile_base_f[:, :, :].rearrange("a i k -> a (i k)")[
                    :, 0:TILES:GROUP_TILES], 0.0, float(N - 1), ALU.max, ALU.min)
                PAD_TILES = TILES - -(-E // TILE_EDGES)
                step(nc.vector.memset(tile_offset_f[:, ITERS - 1, SLOTS - PAD_TILES:SLOTS], 0.0))
                nc.vector.tensor_reduce(offset_span[:, 0:1], tile_offset_f[:, :, :].rearrange("a i k -> a (i k)"),
                                        AX_X, ALU.min)
                step(nc.vector.tensor_reduce(offset_span[:, 1:2], tile_offset_f[:, :, :].rearrange("a i k -> a (i k)"),
                                             AX_X, ALU.max))
                nc.vector.tensor_scalar(offset_over[:, 0:1], offset_span[:, 0:1], 0.0, None, ALU.is_lt)
                nc.vector.tensor_scalar(offset_over[:, 1:2], offset_span[:, 1:2], float(ITER_WINDOW - TILE_WINDOW),
                                        None, ALU.is_gt)
                nc.vector.tensor_scalar(tile_offset[:, :, :], tile_offset_f[:, :, :], 0.0,
                                        float(ITER_WINDOW - TILE_WINDOW), ALU.max, ALU.min).then_inc(offsets_set, 1)

            nc.vector.memset(zeros_wide[:, :], 0.0).then_inc(zeros_wide_set, 1)
            split_low(0)
            split_low(1)
            edge_floats()
            split_low(2)
            local_destinations()
            split_low(3)
            tile_offsets()
            split_low(4)
            for n in (1, 3, 5):
                store_prep(n)
            least_destinations()
            split_low(5)
            relation_biases()
            greatest_destinations()
            split_low(6)
            test_spans()
            for n in (7, 9, 11):
                store_prep(n)
            dve.wait_ge(r_loop_product, 1)
            nc.vector.tensor_copy(r_loop[:, 0:D], psum[0:R, NODE_BANK, P:2 * P])
            dve.wait_ge(over_summed, 1)
            dve.wait_ge(offsets_set, 1)
            step(nc.vector.tensor_reduce(over_sum[:, 0:1], psum[0:1, SUM_BANK, 0:GROUP_BLOCKS * SPANS], AX_X,
                                         ALU.add))
            step(nc.vector.tensor_tensor(over_sum[:, 1:2], over_sum[:, 0:1], offset_over[:, 0:1], ALU.add))
            step(nc.vector.tensor_tensor(over_sum[:, 2:3], over_sum[:, 1:2], offset_over[:, 1:2], ALU.add))
            dve.wait_ge(prep_stored_act, len(PREP) // 2)
            for bank in RING:
                ins = nc.vector.memset(psum[:, bank, JOINT:JOINT + TILE_WINDOW], 0.0)
            step(ins)
            nc.vector.tensor_scalar(general[:, :], over_sum[:, 2:3], 0.5, None, ALU.is_gt).then_inc(general_set, 1)
            step(nc.vector.tensor_tensor(b12_sb[:, :], b1_sb[:, :], b2_sb[:, :], ALU.add))
            dve.wait_ge(prep_stored_act, len(PREP) // 2)

            dve.wait_ge(acc_cleared, 2)

            def make_type_onehot(i, h):
                tiles = slice(h * SLOTS // 2, (h + 1) * SLOTS // 2)
                groups = bass.ds(i * ITER_GROUPS + h * ITER_GROUPS // 2, ITER_GROUPS // 2)
                kind = e_type[:, groups, :].rearrange("p g q -> p (g q)")
                joint = e_joint[:, groups, :].rearrange("p g q -> p (g q)")
                nc.vector.scalar_tensor_tensor(tile_local[:, tiles], kind, -float(TILE_WINDOW), joint,
                                               ALU.mult, ALU.add).then_inc(tile_local_ready, 1)
                nc.vector.tensor_tensor(
                    type_onehot[:, tiles, :], type_iota[:, None, :].to_broadcast([P, SLOTS // 2, R]),
                    kind[:, :, None].to_broadcast([P, SLOTS // 2, R]), ALU.is_equal)

            def make_tile_dst_onehot(i, h):
                tiles = slice(h * SLOTS // 2, (h + 1) * SLOTS // 2)
                dve.wait_ge(tile_local_ready, 2 * i + h + 1)
                nc.vector.tensor_tensor(
                    tile_dst_onehot[:, tiles, :],
                    window_iota[:, None, 0:TILE_WINDOW].to_broadcast([P, SLOTS // 2, TILE_WINDOW]),
                    tile_local[:, tiles, None].to_broadcast([P, SLOTS // 2, TILE_WINDOW]),
                    ALU.is_equal).then_inc(count_onehots_ready, 1)

            def make_dst_onehot(g, hot):
                local = e_local[:, bass.ds(g, 1), :].rearrange("p a q -> p (a q)")
                return nc.vector.tensor_tensor(
                    hot, window_iota[:, None, :].to_broadcast([P, GROUP_TILES, WINDOW]),
                    local[:, :, None].to_broadcast([P, GROUP_TILES, WINDOW]), ALU.is_equal)

            def make_weighted_onehot(i, q):
                g = i * ITER_GROUPS + q
                hot = onehot[:, q, :, :]
                at_least(dve, sums_ready, group_no(i, q) - ITER_GROUPS)
                make_dst_onehot(g, hot).then_inc(onehot_eq, 1)
                weight = e_weight[:, bass.ds(g, 1), :].rearrange("p a q -> p (a q)")
                dve.wait_ge(onehot_eq, g + 1)
                nc.vector.tensor_tensor(hot, hot, weight[:, :, None].to_broadcast([P, GROUP_TILES, WINDOW]),
                                        ALU.mult).then_inc(onehot_ready, 1)

            def load_base(g):
                return nc.values_load_multi_w_load_instructions(
                    group_base[0:1, bass.ds(g, 1)], engines=(mybir.EngineType.DVE,), min_val=0, max_val=N - 1,
                    skip_runtime_bounds_check_because="group_base is clamped to these bounds")[1][0]

            def add_counts(i, s):
                base = load_base(i * ITER_GROUPS)
                dve.wait_ge(tile_added, (i + 1) * SLOTS)
                at_least(dve, iter_counts_added, i)
                near = counts[:, bass.ds(base, ITER_WINDOW)]
                nc.vector.tensor_tensor(near, near, sums[0:R, s, R * ITER_WINDOW:S_COLS],
                                        ALU.add).then_inc(iter_counts_added, 1)

            def add_sums(i, q):
                g = i * ITER_GROUPS + q
                base = load_base(g)
                dve.wait_ge(sums_ready, g + 1)
                at_least(dve, sums_added, g)
                near = acc[:, bass.ds(base, WINDOW)]
                nc.vector.tensor_tensor(near, near, psum[:, q, 0:WINDOW], ALU.add).then_inc(sums_added, 1)

            def iteration(i):
                for q in range(ITER_GROUPS):
                    make_weighted_onehot(i, q)
                    if not isinstance(i, int) or i > 0:
                        add_sums(i - 1, q)

            def load_offsets(i, half):
                row = tile_offset[0:1, bass.ds(i, 1), half * SLOTS // 2:(half + 1) * SLOTS // 2]
                return nc.values_load_multi_w_load_instructions(row.rearrange("a i k -> a (i k)"), engines=(mybir.EngineType.DVE,),
                                            min_val=0, max_val=ITER_WINDOW - TILE_WINDOW,
                    skip_runtime_bounds_check_because="tile_offset is clamped to these bounds")[1]

            def add_tile(i, s, k, offset):
                n = tile_count(i, k)
                dve.wait_ge(tile_sums_ready, n)
                if k == 0:
                    dve.wait_ge(sums_cleared, CLEAR_PARTS * (i + 1))
                at_least(dve, tile_added, n - 1)
                near = sums[:, s, :].rearrange("p (r n) -> p r n", r=BLOCKS)[:, :, bass.ds(offset, TILE_WINDOW)]
                tile_sums = psum[:, tile_bank(k), 0:BLOCKS * TILE_WINDOW].rearrange("p (r n) -> p r n", r=BLOCKS)
                nc.vector.tensor_tensor(near, near, tile_sums, ALU.add).then_inc(tile_added, 1)

            def add_iteration(i):
                base = load_base(i * ITER_GROUPS)
                dve.wait_ge(iter_products_part, CLEAR_PARTS * (i + 1))
                at_least(dve, iter_added, i)
                near = acc[:, bass.ds(base, ITER_WINDOW)]
                nc.vector.tensor_tensor(near, near, psum[:, SUM_BANK, 0:ITER_WINDOW],
                                        ALU.add).then_inc(iter_added, 1)

            def iteration0(i, s, j, last_j):
                first = isinstance(i, int) and i == 0
                for k in range(SLOTS):
                    if k in DVE_ONEHOTS:
                        at_least(dve, tile_sums_ready, tile_count(i, k) - ADD_LAG)
                        key = e_joint[:, :, :].rearrange("p g q -> p (g q)")[:, bass.ds(i * SLOTS + k, 1)]
                        nc.vector.tensor_scalar(joint_onehot[:, k % ADD_LAG, :], joint_iota[:, :], key, None,
                                                ALU.is_equal).then_inc(joint_ready_dve, 1)
                    if k == 0 and not first:
                        offsets = load_offsets(i - 1, 1)
                    if k == ADD_LAG:
                        offsets = load_offsets(i, 0)
                    half, place = divmod(k, SLOTS // 2)
                    if place == 1:
                        at_least(dve, tile_sums_ready, tile_count(i, k + SLOTS // 2 - 2) - SLOTS)
                        make_type_onehot(i, half)
                    if place == 3:
                        make_tile_dst_onehot(i, half)
                    if k == 9 and not first:
                        add_counts(i - 1, 1 - s)
                    if j is not None:
                        if k == 6:
                            dve.wait_ge(iter_added, i - 1)
                            take_agg(j)
                        if k == 10:
                            take_degree(j)
                        if k == 14:
                            degree_reciprocal(j)
                    if last_j is not None:
                        if k == 3:
                            add_residual(last_j)
                        if k in NORM_STEPS:
                            NORM_STEPS[k](0, last_j)
                    if k >= ADD_LAG:
                        add_tile(i, s, k - ADD_LAG, offsets[k - ADD_LAG])
                    elif not first:
                        add_tile(i - 1, 1 - s, k + SLOTS - ADD_LAG, offsets[k])
                    if k == 5 and (not isinstance(i, int) or i >= 2):
                        add_iteration(i - 2)

            def finish0(j):
                last = ITERS - 1
                offsets = load_offsets(last, 1)
                for k in range(ADD_LAG):
                    add_tile(last, 1, k + SLOTS - ADD_LAG, offsets[k])
                    if k == 1:
                        add_residual(j - 1)
                    if 2 <= k < 2 + len(NORM_STEPS):
                        NORM_STEPS[sorted(NORM_STEPS)[k - 2]](0, j - 1)
                add_counts(last, 1)
                add_iteration(last - 1)
                dve.wait_ge(iter_added, last)
                node_tile0(j)
                add_iteration(last)
                dve.wait_ge(iter_added, ITERS)

            def make_messages(i, q):
                g = i * ITER_GROUPS + q
                for k in range(GROUP_TILES):
                    n = g * GROUP_TILES + k
                    slot = q * GROUP_TILES + k
                    dve.wait_ge(gather_done[slot], 16 * (i + 1))
                    nc.vector.tensor_tensor(residual[:, :], gathered_parts[:, slot, 0, :].bitcast(F32),
                                            gathered_parts[:, slot, 1, :].bitcast(F32),
                                            ALU.add).then_inc(parts_summed, 1)
                    dve.wait_ge(message_x_t, n + 1)
                    nc.vector.tensor_copy(agg_t[:, :], node_t).then_inc(message_x_t_ready, 1)
                    message = gathered[:, slot, :]
                    for r in range(R):
                        if r % CHUNK_RELATIONS == 0:
                            dve.wait_ge(products_ready, n * CHUNKS + r // CHUNK_RELATIONS + 1)
                        mask = type_mask[:, r:r + 1]
                        if r == 0:
                            kind = e_type[:, bass.ds(g, 1), k:k + 1].rearrange("p a q -> p (a q)")
                            nc.vector.tensor_scalar(type_mask[:, :], type_iota[:, :], kind, None,
                                                    ALU.is_equal).then_inc(mask_ready, 1)
                            dve.wait_ge(mask_ready, n + 1)
                        product = psum[:, r // CHUNK_RELATIONS % 2, r % CHUNK_RELATIONS * D:
                                       (r % CHUNK_RELATIONS + 1) * D]
                        if r == 0:
                            ins = nc.vector.tensor_scalar(message, product, mask, None, ALU.mult)
                        else:
                            dve.wait_ge(message_step, n * R + r)
                            ins = nc.vector.scalar_tensor_tensor(message, product, mask, message,
                                                                 ALU.mult, ALU.add)
                        ins.then_inc(message_step, 1)
                dve.wait_ge(message_step, (g + 1) * GROUP_TILES * R)
                dve.nop(nofuse=True)

            def general_iteration(layer, i):
                for q in range(ITER_GROUPS):
                    g = i * ITER_GROUPS + q
                    if layer == 0:
                        make_messages(i, q)
                        kind = e_type[:, bass.ds(g, 1), :].rearrange("p a q -> p (a q)")
                        nc.vector.tensor_tensor(
                            type_onehot[:, 0:GROUP_TILES, 0:R],
                            type_iota[:, None, :].to_broadcast([P, GROUP_TILES, R]),
                            kind[:, :, None].to_broadcast([P, GROUP_TILES, R]), ALU.is_equal)

                    def window(w):
                        n = (layer * GROUPS + g) * WINDOWS + w
                        where = e_dst[:, bass.ds(g, 1), :].rearrange("p a q -> p (a q)")
                        if isinstance(w, int) and w == 0:
                            nc.vector.tensor_copy(rel_dst[:, :], where).then_inc(gen_rel, 1)
                        else:
                            nc.vector.tensor_scalar(rel_dst[:, :], rel_dst[:, :], -float(WINDOW), None,
                                                    ALU.add).then_inc(gen_rel, 1)
                        dve.wait_ge(gen_rel, n + 1)
                        hot = onehot[:, 0, :, :]
                        if layer == 0:
                            nc.vector.tensor_tensor(
                                dst_onehot[:, :, :],
                                window_iota[:, None, :].to_broadcast([P, GROUP_TILES, WINDOW]),
                                rel_dst[:, :, None].to_broadcast([P, GROUP_TILES, WINDOW]), ALU.is_equal)
                        nc.vector.tensor_tensor(
                            hot, window_iota[:, None, :].to_broadcast([P, GROUP_TILES, WINDOW]),
                            rel_dst[:, :, None].to_broadcast([P, GROUP_TILES, WINDOW]), ALU.is_equal
                        ).then_inc(gen_eq, 1)
                        dve.wait_ge(gen_eq, n + 1)
                        if layer == 0:
                            nc.vector.tensor_scalar(rel_dst[:, :], rel_dst[:, :], 0.0, None,
                                                    ALU.add).then_inc(gen_onehot_ready, 1)
                        else:
                            weight = e_weight[:, bass.ds(g, 1), :].rearrange("p a q -> p (a q)")
                            nc.vector.tensor_tensor(hot, hot,
                                                    weight[:, :, None].to_broadcast([P, GROUP_TILES, WINDOW]),
                                                    ALU.mult).then_inc(gen_onehot_ready, 1)
                        dve.wait_ge(gen_sum_ready, n + 1)
                        if layer == 0:
                            near = counts[:, bass.ds(w * WINDOW, WINDOW)]
                            nc.vector.tensor_tensor(near, near, count_sums, ALU.add)
                        near = acc[:, bass.ds(w * WINDOW, WINDOW)]
                        nc.vector.tensor_tensor(near, near, psum[:, 0, 0:WINDOW], ALU.add).then_inc(gen_added, 1)
                        dve.wait_ge(gen_added, n + 1)
                        dve.nop(nofuse=True)

                    window(0)
                    with dve.Fori(1, WINDOWS - 1) as w:
                        window(w)
                    window(WINDOWS - 1)
                    dve.wait_ge(counts_ready if layer == 0 else sums_ready, group_no(i, q))
                    dve.nop(nofuse=True)
                    added = counts_added if layer == 0 else sums_added
                    nc.vector.tensor_copy(rel_dst[:, :], e_dst[:, bass.ds(g, 1), :].rearrange("p a q -> p (a q)")
                                          ).then_inc(added, 1)
                    dve.wait_ge(added, group_no(i, q))

            def norm_stats(layer, j):
                n = tile_no(layer, j)
                dve.wait_ge(residual_ready, n)
                nc.vector.bn_stats(bn[:, :], residual[:, :]).then_inc(bn_ready, 1)

            def norm_mean_var(layer, j):
                dve.wait_ge(bn_ready, tile_no(layer, j))
                dve.nop(nofuse=True)
                nc.vector.bn_aggr(mean_var, bn[:, :]).then_inc(mean_var_ready, 1)

            def norm_eps(layer, j):
                dve.wait_ge(mean_var_ready, tile_no(layer, j))
                nc.vector.tensor_scalar(var_eps, mean_var[:, 1:2], LN_EPS, None, ALU.add).then_inc(var_eps_ready, 1)

            def norm_reciprocal(layer, j):
                dve.wait_ge(std_ready, tile_no(layer, j))
                nc.vector.reciprocal(rstd, std).then_inc(rstd_ready, 1)

            def norm_result(layer, j):
                dve.wait_ge(rstd_ready, tile_no(layer, j))
                at_least(dve, x1_stored if layer == 0 else out_stored, 16 * j)
                nc.vector.tensor_scalar(result[:, :], residual[:, :], mean_var[:, 0:1], rstd,
                                        ALU.subtract, ALU.mult).then_inc(result_ready, 1)

            NORM_STEPS = {5: norm_stats, 7: norm_mean_var, 9: norm_eps, 13: norm_reciprocal, 15: norm_result}

            def layer_norm(layer, j):
                for k in sorted(NORM_STEPS):
                    NORM_STEPS[k](layer, j)

            def take_agg(j):
                at_least(dve, proj_ready, j)
                dve.nop(nofuse=True)
                nc.vector.tensor_copy(agg_t[:, :], acc[:, bass.ds(j * P, P)]).then_inc(agg_ready, 1)

            def take_degree(j):
                dve.wait_ge(proj_ready, j + 1)
                nc.vector.tensor_scalar(degree, node_degree, 1.0, None, ALU.max).then_inc(degree_ready, 1)

            def degree_reciprocal(j):
                dve.wait_ge(root_ready, j + 1)
                nc.vector.reciprocal(degree_norm, degree_root).then_inc(norm_ready, 1)

            def add_residual(j):
                dve.wait_ge(activated_ready, j + 1)
                dve.wait_ge(node_loaded, 16 * (j + 1))
                nc.vector.tensor_tensor(residual[:, :], activated[:, :], node_x[:, :],
                                        ALU.add).then_inc(residual_ready, 1)

            def node_tile0(j):
                take_agg(j)
                take_degree(j)
                degree_reciprocal(j)
                add_residual(j)
                layer_norm(0, j)

            def node_tile1(j):
                n = tile_no(1, j)
                cols = acc[:, bass.ds(j * P, P)]
                dve.wait_ge(node_t_ready, j + 1)
                at_least(dve, proj_ready, n - 1)
                nc.vector.tensor_tensor(agg_t[:, :], cols, node_t, ALU.add)
                nc.vector.tensor_tensor(product_t[:, :], cols, node_t,
                                        ALU.mult).then_inc(agg_ready, 1)
                dve.wait_ge(sloped_ready, j + 1)
                nc.vector.tensor_tensor(activated[:, :], node_proj, squares[:, :],
                                        ALU.max).then_inc(leaky_ready, 1)
                dve.wait_ge(length_ready, j + 1)
                nc.vector.tensor_scalar(length_floor, length, NORM_EPS, None, ALU.max).then_inc(length_floored, 1)
                dve.wait_ge(length_floored, j + 1)
                nc.vector.reciprocal(inv_length, length_floor).then_inc(inv_length_ready, 1)
                dve.wait_ge(inv_length_ready, j + 1)
                nc.vector.scalar_tensor_tensor(residual[:, :], activated[:, :], inv_length, node_x[:, :],
                                               ALU.mult, ALU.add).then_inc(residual_ready, 1)
                layer_norm(1, j)

            def finish1():
                for q in range(ITER_GROUPS):
                    add_sums(ITERS - 1, q)
                dve.wait_ge(sums_added, GROUPS)

            fast_or_general(dve, nc.vector,
                            lambda: run_fast_pairs(dve, LAGS[0], iteration0, node_tile0, finish0),
                            lambda: run_general(dve, lambda i: general_iteration(0, i), node_tile0))
            dve.wait_ge(acc_cleared, 4)
            fast_or_general(dve, nc.vector,
                            lambda: run_fast(dve, LAGS[1], iteration, node_tile1, finish1),
                            lambda: run_general(dve, lambda i: general_iteration(1, i), node_tile1))

        @block.tensor
        def _(pe):
            pe.wait_ge(consts_set, 7)
            pe.wait_ge(floats_ready, 1)
            for n, (a, b) in enumerate(PREP):
                at_least(pe, prep_stored_dve if n % 2 else prep_stored_act, (n - 8) // 2 + 1)
                for q in range(GROUP_TILES):
                    ins = nc.tensor.transpose(psum[:, n % 8, q * P:(q + 1) * P],
                                              prep_in[a][b][:, q * P:(q + 1) * P], identity[:, :])
                ins.then_inc(prep_transposed, 1)
            pe.wait_ge(weights_in, 16 * 6)
            pe.wait_ge(prep_stored_act, 4)
            nc.tensor.transpose(psum[:, NODE_BANK, 0:R], r_feat[:, :], identity[0:R, 0:R]).then_inc(r_feat_transposed, 1)
            pe.wait_ge(loop_plus_ready, 1)
            nc.tensor.matmul(psum[0:R, NODE_BANK, P:2 * P], r_feat_t[:, :], loop_plus_i[:, 0:D],
                             start=True, stop=True).then_inc(r_loop_product, 1)
            pe.wait_ge(over_ready, 1)
            pe.wait_ge(prep_stored_act, len(PREP) // 2)
            pe.wait_ge(prep_stored_dve, len(PREP) // 2)
            nc.tensor.matmul(psum[0:1, SUM_BANK, 0:GROUP_BLOCKS * SPANS], ones[:, 0:1],
                             span_over[:, :, :].rearrange("p b s -> p (b s)"), start=True, stop=True
                             ).then_inc(over_summed, 1)
            pe.wait_ge(general_set, 1)

            def group_sums(k0, hot, slots_ready):
                bank = k0 // GROUP_TILES
                for k in range(GROUP_TILES):
                    slots_ready(k0 + k)
                    ins = nc.tensor.matmul(psum[:, bank, 0:WINDOW], gathered[:, k0 + k, :], hot[:, k, :],
                                           start=(k == 0), stop=(k == GROUP_TILES - 1))
                return ins

            def tile_counts(k):
                nc.tensor.matmul(psum[0:R, tile_bank(k), JOINT:JOINT + TILE_WINDOW], type_onehot[:, k, :],
                                 tile_dst_onehot[:, k, :], start=True, stop=True)

            def tile_sums(k):
                for part in range(2):
                    ins = nc.tensor.matmul(psum[:, tile_bank(k), 0:JOINT], gathered_parts[:, k, part, :],
                                           joint_onehot[:, k % ADD_LAG, :], start=(part == 0), stop=(part == 1))
                return ins

            def iteration(i):
                for q in range(ITER_GROUPS):
                    pe.wait_ge(onehot_ready, group_no(i, q))
                    at_least(pe, sums_added, group_no(i, q) - ITER_GROUPS)
                    group_sums(q * GROUP_TILES, onehot[:, q, :, :],
                               lambda k: pe.wait_ge(gather_done[k], 16 * (ITERS + i + 1))).then_inc(sums_ready, 1)

            def relations(i, s, r0, r1):
                for r in range(r0, r1):
                    ins = nc.tensor.matmul(psum[:, SUM_BANK, 0:ITER_WINDOW], relation_w[:, r * D:(r + 1) * D],
                                           sums[:, s, r * ITER_WINDOW:(r + 1) * ITER_WINDOW],
                                           start=(r == 0), stop=(r == R - 1))
                    if (r + 1) % (R // CLEAR_PARTS) == 0:
                        ins.then_inc(iter_products_part, 1)

            def iteration0(i, s, j, last_j):
                first = isinstance(i, int) and i == 0
                if isinstance(i, int) and i == 1:
                    pe.wait_ge(relation_w_in, 16)
                relation = 0
                for k in range(SLOTS):
                    if j is not None and k == 1:
                        node_tile0(j)
                    if k % (SLOTS // 2) == 0:
                        pe.wait_ge(count_onehots_ready, 2 * i + k // (SLOTS // 2) + 1)
                    if k % 2 == 0:
                        at_least(pe, tile_added, tile_count(i, k + 1) - tiles_back(k + 1))
                        tile_counts(k)
                        tile_counts(k + 1)
                    pe.wait_ge(gather_done[k], 16 * (i + 1))
                    if k in ACT_ONEHOTS:
                        pe.wait_ge(joint_ready_act, i * len(ACT_ONEHOTS) + ACT_ONEHOTS.index(k) + 1)
                    else:
                        pe.wait_ge(joint_ready_dve, i * len(DVE_ONEHOTS) + DVE_ONEHOTS.index(k) + 1)
                    tile_sums(k).then_inc(tile_sums_ready, 1)
                    if not first and k in RELATIONS_BEHIND:
                        if relation == 0:
                            pe.wait_ge(tile_added, i * SLOTS)
                            at_least(pe, iter_added, i - 1)
                        relations(i - 1, 1 - s, relation, relation + RELATIONS_BEHIND[k])
                        relation += RELATIONS_BEHIND[k]

            def finish0(j):
                node_tile0(j)
                pe.wait_ge(tile_added, TILES)
                pe.wait_ge(iter_added, ITERS - 1)
                relations(ITERS - 1, 1, 0, R)

            def messages(i, q):
                for k in range(GROUP_TILES):
                    n = (i * ITER_GROUPS + q) * GROUP_TILES + k
                    pe.wait_ge(parts_summed, n + 1)
                    nc.tensor.transpose(node_t, residual[:, :], identity[:, :]
                                        ).then_inc(message_x_t, 1)
                    pe.wait_ge(message_x_t_ready, n + 1)
                    for c in range(CHUNKS):
                        at_least(pe, message_step, n * R + (c - 1) * CHUNK_RELATIONS)
                        nc.tensor.matmul(psum[:, c % 2, :], agg_t[:, :], relation_w[:, c * BANK:(c + 1) * BANK],
                                         start=True, stop=True).then_inc(products_ready, 1)
                pe.wait_ge(message_step, (i * ITER_GROUPS + q + 1) * GROUP_TILES * R)

            def general_iteration(layer, i):
                if isinstance(i, int) and layer == 0:
                    pe.wait_ge(relation_w_in, 16)
                for q in range(ITER_GROUPS):
                    g = i * ITER_GROUPS + q
                    for k in range(q * GROUP_TILES, (q + 1) * GROUP_TILES):
                        pe.wait_ge(gather_done[k], 16 * (layer * ITERS + i + 1))
                    if layer == 0:
                        messages(i, q)

                    def window(w):
                        n = (layer * GROUPS + g) * WINDOWS + w
                        pe.wait_ge(gen_onehot_ready, n + 1)
                        at_least(pe, gen_added, n)
                        for k in range(GROUP_TILES):
                            ins = nc.tensor.matmul(psum[:, 0, 0:WINDOW], gathered[:, q * GROUP_TILES + k, :],
                                                   onehot[:, 0, k, :], start=(k == 0),
                                                   stop=(k == GROUP_TILES - 1))
                        if layer == 0:
                            for k in range(GROUP_TILES):
                                ins = nc.tensor.matmul(count_sums, type_onehot[:, k, 0:R], dst_onehot[:, k, :],
                                                       start=(k == 0), stop=(k == GROUP_TILES - 1))
                        ins.then_inc(gen_sum_ready, 1)

                    window(0)
                    with pe.Fori(1, WINDOWS - 1) as w:
                        window(w)
                    window(WINDOWS - 1)
                    nc.tensor.matmul(psum[:, 1, 0:WINDOW], gathered[:, q * GROUP_TILES, :], onehot[:, 0, 0, :],
                                     start=True, stop=True).then_inc(counts_ready if layer == 0 else sums_ready, 1)
                    if layer == 0:
                        nc.tensor.matmul(psum[:, 2, 0:WINDOW], gathered[:, q * GROUP_TILES, :],
                                         onehot[:, 0, 0, :], start=True, stop=True).then_inc(tile_sums_ready, GROUP_TILES)

            def node_tile0(j):
                pe.wait_ge(count_tile_ready, j + 1)
                pe.wait_ge(agg_ready, j + 1)
                at_least(pe, activated_ready, j)
                proj_degree = psum[:, NODE_BANK, 0:D + 1]
                nc.tensor.matmul(proj_degree, count_tile[:, :], r_loop[:, :], start=True, stop=False)
                nc.tensor.matmul(proj_degree, agg_t[:, :], loop_plus_i[:, :],
                                 start=False, stop=True).then_inc(proj_ready, 1)

            def node_tile1(j):
                n = tile_no(1, j)
                pe.wait_ge(node_loaded, 16 * n)
                pe.wait_ge(activated_ready, NODE_TILES)
                at_least(pe, leaky_ready, j)
                nc.tensor.transpose(node_t, node_x[:, :], identity[:, :]).then_inc(node_t_ready, 1)
                pe.wait_ge(agg_ready, n)
                nc.tensor.matmul(node_proj, agg_t[:, :], w1_sb[:, :], start=True, stop=False)
                nc.tensor.matmul(node_proj, product_t[:, :], w2_sb[:, :], start=False, stop=False)
                nc.tensor.matmul(node_proj, ones[0:1, :], b12_sb[:, :],
                                 start=False, stop=True).then_inc(proj_ready, 1)

            fast_or_general(pe, nc.tensor,
                            lambda: run_fast_pairs(pe, LAGS[0], iteration0, node_tile0, finish0),
                            lambda: run_general(pe, lambda i: general_iteration(0, i), node_tile0))
            fast_or_general(pe, nc.tensor,
                            lambda: run_fast(pe, LAGS[1], iteration, node_tile1, lambda: None, tile_first=True),
                            lambda: run_general(pe, lambda i: general_iteration(1, i), node_tile1))


_INS = ["x", "src", "dst", "edge_type_40", "edge_weight", "L0_gnn_rFeatures", "L0_gnn_relation_weights",
        "L0_gnn_loop_weight", "L1_gnn_W1", "L1_gnn_W2", "L1_gnn_b1", "L1_gnn_b2"]


def kernel(**inputs):
    import numpy as _np
    import concourse.bacc as _bacc
    from concourse import mybir as _mybir
    from concourse.bass_utils import run_bass_kernel_spmd as _run

    nc = _bacc.Bacc("TRN2", target_bir_lowering=False, num_devices=1)
    arrays, args = {}, []
    for name in _INS:
        a = _np.ascontiguousarray(inputs[name])
        arrays[f"in_{name}_dram"] = a
        args.append(nc.dram_tensor(f"in_{name}_dram", a.shape, _mybir.dt.from_np(a.dtype), kind="ExternalInput").ap())
    shape = inputs["x"].shape
    args.append(nc.dram_tensor("out_dram", shape, _mybir.dt.float32, kind="ExternalOutput").ap())
    build(nc, *args)
    r = _run(nc, [arrays], core_ids=[0])
    return r.results[0]["out_dram"]
```
